# Optimizing a Trainium2 kernel written in Bass

```python
import numpy as np
import jax
import jax.numpy as jnp

def _softmax(x, axis=-1):
    return jax.nn.softmax(x, axis=axis)

def _gelu(x):
    return jax.nn.gelu(x, approximate=True)

def _silu(x):
    return jax.nn.silu(x)

def _sigmoid(x):
    return jax.nn.sigmoid(x)

def _layernorm(x, axis=-1, eps=1e-05):
    m = jnp.mean(x, axis=axis, keepdims=True)
    v = jnp.var(x, axis=axis, keepdims=True)
    return (x - m) / jnp.sqrt(v + eps)

def _scatter_add(tgt, idx, src, axis=0):
    return tgt.at[idx].add(src)

def _segment_sum(src, seg, n):
    return jax.ops.segment_sum(src, seg, n)
kernel_name = 'mk_xattn_ffn_d1_seqx_r8_64060f'

def setup_inputs(seed: int=0):
    np.random.seed(seed)
    _w = jnp.asarray

    def _rec_inputs():
        import jax
        import jax.numpy as jnp
        _rk = jax.random.key(seed)
        x = -0.0003929 + 0.9999 * jax.random.normal(jax.random.fold_in(_rk, 1), (32, 64, 512), jnp.float32)
        _lenS = 64 - jax.random.randint(jax.random.fold_in(_rk, 7), (32,), 0, max(1, 64 // 4) + 1, jnp.int32)
        _lenS2 = 64 - jax.random.randint(jax.random.fold_in(_rk, 8), (32,), 0, max(1, 64 // 4) + 1, jnp.int32)
        _ctx_4096P = jax.random.normal(jax.random.fold_in(_rk, 11), (32, 16, 512), jnp.float32)
        _ctx_4096c = jax.random.dirichlet(jax.random.fold_in(_rk, 511), 0.3 * jnp.ones((16,), jnp.float32), (32, 64))
        _ctx_4096t = jnp.einsum('bsk,bkd->bsd', _ctx_4096c, _ctx_4096P)
        _ctx_4096t = _ctx_4096t * jax.lax.rsqrt(jnp.mean(jnp.square(_ctx_4096t)) + 1e-12) * 0.953939
        ctx_4096 = 2.81802e-05 + 1.00001 * (_ctx_4096t + 0.3 * jax.random.normal(jax.random.fold_in(_rk, 611), (32, 64, 512), jnp.float32))
        pos_BxS2 = jnp.broadcast_to(jnp.arange(64, dtype=jnp.int32), (32, 64))
        _validS = jnp.arange(64)[None, :] < _lenS[:, None]
        _validS2 = jnp.arange(64)[None, :] < _lenS2[:, None]
        _causal = jnp.tril(jnp.ones((64, 64), dtype=bool))
        mask_BxSxS2_ik0 = jnp.where(jnp.broadcast_to(_validS2[:, None, :], (32, 64, 64)), 0, 1).astype(jnp.int32)
        return (x, ctx_4096, pos_BxS2, mask_BxSxS2_ik0)
    x, ctx_4096, pos_BxS2, mask_BxSxS2_ik0 = _rec_inputs()

    def _L0_xattn_setup():
        import jax, jax.numpy as jnp
        import numpy as np
        B, S, E = (2, 256, 512)
        H, KVH, D = (32, 8, 128)
        GROUPS = H // KVH
        MAX_POS = 512
        ROPE_THETA = 10000.0

        def _rope_tables(max_pos, dim, theta):
            inv_freq = 1.0 / theta ** (jnp.arange(0, dim, 2, dtype=jnp.float32) / dim)
            t = jnp.arange(max_pos, dtype=jnp.float32)
            freqs = jnp.einsum('i,j->ij', t, inv_freq)
            emb = jnp.concatenate([freqs, freqs], axis=-1)
            return (jnp.cos(emb), jnp.sin(emb))

        def _rotate_half(x):
            x1, x2 = (x[..., :x.shape[-1] // 2], x[..., x.shape[-1] // 2:])
            return jnp.concatenate([-x2, x1], axis=-1)
        key = jax.random.key(seed)
        ks = jax.random.split(key, 8)
        scale_w = 1.0 / np.sqrt(E)
        query = jax.random.normal(ks[0], (B, S, E), dtype=jnp.float32)
        k_in = jax.random.normal(ks[1], (B, S, E), dtype=jnp.float32)
        v_in = jax.random.normal(ks[2], (B, S, E), dtype=jnp.float32)
        position_ids = jnp.broadcast_to(jnp.arange(S, dtype=jnp.int64), (B, S))
        src_mask = jnp.tril(jnp.ones((S, S), dtype=jnp.int32))
        src_mask = jnp.broadcast_to(src_mask, (B, S, S))
        Wq = jax.random.normal(ks[3], (E, H * D), dtype=jnp.float32) * scale_w
        Wk = jax.random.normal(ks[4], (E, KVH * D), dtype=jnp.float32) * scale_w
        Wv = jax.random.normal(ks[5], (E, KVH * D), dtype=jnp.float32) * scale_w
        Wo = jax.random.normal(ks[6], (H * D, E), dtype=jnp.float32) * scale_w
        return {'query': query, 'key': k_in, 'value': v_in, 'position_ids': position_ids, 'src_mask': src_mask, 'Wq': Wq, 'Wk': Wk, 'Wv': Wv, 'Wo': Wo}
    _L0_xattn_all = _L0_xattn_setup()
    _L0_xattn_in = {k: v for k, v in _L0_xattn_all.items() if k in ('Wq', 'Wk', 'Wv', 'Wo')}
    del _L0_xattn_all

    def _L0_ffn_setup():
        import jax, jax.numpy as jnp
        import numpy as np
        BLOCK_SIZE = 32
        FP4_VALUES = jnp.array([0.0, 0.5, 1.0, 1.5, 2.0, 3.0, 4.0, 6.0], dtype=jnp.float32)
        FP4_BOUNDS = jnp.array([0.25, 0.75, 1.25, 1.75, 2.5, 3.5, 5.0], dtype=jnp.float32)
        FP4_MAX = 6.0

        def quantize_to_mxfp4(w, block_size):
            K, N = w.shape
            wb = w.reshape(K // block_size, block_size, N)
            amax = jnp.max(jnp.abs(wb), axis=1, keepdims=True)
            scale = jnp.exp2(jnp.ceil(jnp.log2(jnp.maximum(amax, 1e-30) / FP4_MAX)))
            scaled = wb / scale
            mag_idx = jnp.searchsorted(FP4_BOUNDS, jnp.abs(scaled)).astype(jnp.uint8)
            sign = (scaled < 0).astype(jnp.uint8)
            codes = mag_idx | sign << 3
            packed = codes[:, 1::2, :] << 4 | codes[:, 0::2, :]
            return (packed, scale[:, 0, :])

        def dequantize_mxfp4(packed, scales, block_size):
            Kb, half_b, N = packed.shape
            low = packed & 15
            high = packed >> 4
            codes = jnp.stack([low, high], axis=2).reshape(Kb, block_size, N)
            mag = FP4_VALUES[(codes & 7).astype(jnp.int32)]
            sgn = jnp.where(codes >> 3 > 0, -1.0, 1.0)
            wb = sgn * mag * scales[:, None, :]
            return wb.reshape(Kb * block_size, N)

        def mxfp4_matmul(x, packed, scales, block_size):
            w = dequantize_mxfp4(packed, scales, block_size)
            return jnp.einsum('...k,kn->...n', x, w)
        key = jax.random.key(seed)
        k1, k2 = jax.random.split(key)
        B, S, K, N = (4, 256, 512, 512)
        inputs = jax.random.normal(k1, (B, S, K), dtype=jnp.float32)
        kernel = jax.random.normal(k2, (K, N), dtype=jnp.float32) * K ** (-0.5)
        bias = jnp.zeros((N,), dtype=jnp.float32)
        return {'inputs': inputs, 'kernel': kernel, 'bias': bias}
    _L0_ffn_all = _L0_ffn_setup()
    _L0_ffn_in = {k: v for k, v in _L0_ffn_all.items() if k in ('kernel', 'bias')}
    del _L0_ffn_all
    return {'x': x, 'ctx_4096': ctx_4096, 'pos_BxS2': pos_BxS2, 'mask_BxSxS2_ik0': mask_BxSxS2_ik0, 'L0_xattn_Wq': _L0_xattn_in['Wq'], 'L0_xattn_Wk': _L0_xattn_in['Wk'], 'L0_xattn_Wv': _L0_xattn_in['Wv'], 'L0_xattn_Wo': _L0_xattn_in['Wo'], 'L0_ffn_kernel': _L0_ffn_in['kernel'], 'L0_ffn_bias': _L0_ffn_in['bias']}

def reference(x, ctx_4096, pos_BxS2, mask_BxSxS2_ik0, L0_xattn_Wq, L0_xattn_Wk, L0_xattn_Wv, L0_xattn_Wo, L0_ffn_kernel, L0_ffn_bias):
    import jax
    import jax.numpy as jnp

    def _L0_xattn_ref(query, key, value, position_ids, src_mask, Wq, Wk, Wv, Wo):
        import jax, jax.numpy as jnp
        import numpy as np
        B, S, E = (2, 256, 512)
        H, KVH, D = (32, 8, 128)
        GROUPS = H // KVH
        MAX_POS = 512
        ROPE_THETA = 10000.0

        def _rope_tables(max_pos, dim, theta):
            inv_freq = 1.0 / theta ** (jnp.arange(0, dim, 2, dtype=jnp.float32) / dim)
            t = jnp.arange(max_pos, dtype=jnp.float32)
            freqs = jnp.einsum('i,j->ij', t, inv_freq)
            emb = jnp.concatenate([freqs, freqs], axis=-1)
            return (jnp.cos(emb), jnp.sin(emb))

        def _rotate_half(x):
            x1, x2 = (x[..., :x.shape[-1] // 2], x[..., x.shape[-1] // 2:])
            return jnp.concatenate([-x2, x1], axis=-1)
        nb, q_len, _ = query.shape
        q = (query @ Wq).reshape(nb, q_len, H, D).transpose(0, 2, 1, 3)
        k = (key @ Wk).reshape(nb, q_len, KVH, D).transpose(0, 2, 1, 3)
        v = (value @ Wv).reshape(nb, q_len, KVH, D).transpose(0, 2, 1, 3)
        cos_t, sin_t = _rope_tables(MAX_POS, D, ROPE_THETA)
        cos = cos_t[position_ids][:, None]
        sin = sin_t[position_ids][:, None]
        q = q * cos + _rotate_half(q) * sin
        k = k * cos + _rotate_half(k) * sin
        k = jnp.repeat(k, GROUPS, axis=1)
        v = jnp.repeat(v, GROUPS, axis=1)
        scores = jnp.einsum('bhqd,bhkd->bhqk', q, k) / jnp.sqrt(jnp.float32(D))
        mask = src_mask[:, None]
        scores = jnp.where(mask == 0, jnp.float32(-1000000000.0), scores)
        attn = jax.nn.softmax(scores, axis=-1)
        x = jnp.einsum('bhqk,bhkd->bhqd', attn, v)
        x = x.transpose(0, 2, 1, 3).reshape(nb, q_len, H * D)
        return x @ Wo

    def _L0_ffn_ref(inputs, kernel, bias):
        import jax, jax.numpy as jnp
        import numpy as np
        BLOCK_SIZE = 32
        FP4_VALUES = jnp.array([0.0, 0.5, 1.0, 1.5, 2.0, 3.0, 4.0, 6.0], dtype=jnp.float32)
        FP4_BOUNDS = jnp.array([0.25, 0.75, 1.25, 1.75, 2.5, 3.5, 5.0], dtype=jnp.float32)
        FP4_MAX = 6.0

        def quantize_to_mxfp4(w, block_size):
            K, N = w.shape
            wb = w.reshape(K // block_size, block_size, N)
            amax = jnp.max(jnp.abs(wb), axis=1, keepdims=True)
            scale = jnp.exp2(jnp.ceil(jnp.log2(jnp.maximum(amax, 1e-30) / FP4_MAX)))
            scaled = wb / scale
            mag_idx = jnp.searchsorted(FP4_BOUNDS, jnp.abs(scaled)).astype(jnp.uint8)
            sign = (scaled < 0).astype(jnp.uint8)
            codes = mag_idx | sign << 3
            packed = codes[:, 1::2, :] << 4 | codes[:, 0::2, :]
            return (packed, scale[:, 0, :])

        def dequantize_mxfp4(packed, scales, block_size):
            Kb, half_b, N = packed.shape
            low = packed & 15
            high = packed >> 4
            codes = jnp.stack([low, high], axis=2).reshape(Kb, block_size, N)
            mag = FP4_VALUES[(codes & 7).astype(jnp.int32)]
            sgn = jnp.where(codes >> 3 > 0, -1.0, 1.0)
            wb = sgn * mag * scales[:, None, :]
            return wb.reshape(Kb * block_size, N)

        def mxfp4_matmul(x, packed, scales, block_size):
            w = dequantize_mxfp4(packed, scales, block_size)
            return jnp.einsum('...k,kn->...n', x, w)
        packed, scales = quantize_to_mxfp4(kernel, BLOCK_SIZE)
        y = mxfp4_matmul(inputs, packed, scales, BLOCK_SIZE)
        return y + bias
    x = x + _L0_xattn_ref(_layernorm(x, axis=-1), ctx_4096, ctx_4096, pos_BxS2, mask_BxSxS2_ik0, L0_xattn_Wq, L0_xattn_Wk, L0_xattn_Wv, L0_xattn_Wo)
    x = x + _L0_ffn_ref(_layernorm(x, axis=-1), L0_ffn_kernel, L0_ffn_bias)
    return x

_drawn_inputs = setup_inputs


def setup_inputs(seed=0):
    import zlib

    import numpy as np

    out = dict(_drawn_inputs(seed))
    spreads = {'L0_ffn_bias': (0.0, 0.1)}
    factors = {}
    for name, (base, spread) in spreads.items():
        noise = np.random.default_rng([zlib.crc32(name.encode()), seed]).standard_normal(out[name].shape)
        drawn = base * np.exp(spread * noise) if base else spread * noise
        out[name] = jnp.asarray(drawn.astype(out[name].dtype))
    for name, factor in factors.items():
        out[name] = (out[name] * factor).astype(out[name].dtype)
    return out
```

```python
from contextlib import ExitStack

import numpy as np

import concourse.bass as bass
from concourse import mybir

F32 = mybir.dt.float32
F32R = mybir.dt.float32r
BF16 = mybir.dt.bfloat16
FP16 = mybir.dt.float16
I32 = mybir.dt.int32
U32 = mybir.dt.uint32
U8 = mybir.dt.uint8
ALU = mybir.AluOpType
ACT = mybir.ActivationFunctionType
AX = mybir.AxisListType

HALVES = 2
GROUPS = 8
CHUNKS = 2
STEPS = HALVES * GROUPS * CHUNKS
PAIRS = 4 * STEPS
HALF = 8 * GROUPS
RAW = 3
WO_RING = 6
PROJ = 3
SCALE = float(1.0 / np.sqrt(np.float32(128.0)))
FIRST = -4


class Queue:

    def __init__(self, sem):
        self.sem, self.count, self.items = sem, 0, []

    def add(self, made, fn, *waits):
        self.items.append((fn, waits, made))


class Program:

    def __init__(self):
        self.at = {}
        self.prod = {}

    def done_by(self, queue, name):
        queue.count += 1
        assert name not in self.at, name
        self.at[name] = (queue.sem, queue.count)

    def issue(self, queue, eng):
        seen = {}
        for fn, waits, made in queue.items:
            for name in waits:
                if name is None:
                    continue
                sem, value = self.at[name]
                if seen.get(id(sem), 0) < value:
                    eng.wait_ge(sem, value)
                    seen[id(sem)] = value
            ins = fn(eng)
            if made is not None and ins is not None:
                ins.then_inc(queue.sem, 1)


def group_of(step):
    return (step // CHUNKS) % GROUPS


def build(nc, x, ctxT, pos, mask, wq, wk, wv, wo, fkT, fbias, table, eye, out):
    ctx = ExitStack()
    with ctx:
        def sb(name, shape, dt):
            return ctx.enter_context(nc.sbuf_tensor(name, shape, dt))

        def pb(name, shape):
            return ctx.enter_context(nc.psum_tensor(name, shape, F32))

        def sem(name):
            return ctx.enter_context(nc.semaphore(name))

        XH, XL = sb("XH", [128, 4, 1024], F32R), sb("XL", [128, 4, 1024], F32R)
        CH, CL = sb("CH", [128, 4, 1024], F32R), sb("CL", [128, 4, 1024], F32R)
        acc = sb("acc", [128, 8, 512], F32)
        COS, SIN = sb("COS", [128, 1024], F32), sb("SIN", [128, 1024], F32)
        qT = sb("qT", [128, 2, 8, 4, 64], F32)
        kT = sb("kT", [128, 2, 512], F32)
        VH, VL = sb("VH", [128, 8, 256], F32R), sb("VL", [128, 8, 256], F32R)
        QH, QL = sb("QH", [128, 4, 4, 128], F32R), sb("QL", [128, 4, 4, 128], F32R)
        KH, KL = sb("KH", [128, 4, 128], F32R), sb("KL", [128, 4, 128], F32R)
        UH, UL = sb("UH", [128, 4, 256], F32R), sb("UL", [128, 4, 256], F32R)
        OH, OL = sb("OH", [128, WO_RING, 512], F32R), sb("OL", [128, WO_RING, 512], F32R)
        raw = sb("raw", [128, RAW, 512], F32)
        AH, AL = sb("AH", [128, 2, 4, 128], F32R), sb("AL", [128, 2, 4, 128], F32R)
        t2 = sb("t2", [128, 512], F32)
        sm = sb("sm", [128, 2, 256], F32)
        PH, PL = sb("PH", [128, 256], F32R), sb("PL", [128, 256], F32R)
        ident = sb("ident", [128, 128], F32)
        mk = sb("mk", [128, 8, 128], U8)
        W4 = sb("W4", [128, 4, 512], BF16)
        bias = sb("bias", [128, 512], F32)
        FH, FL = sb("FH", [128, 4, 128], FP16), sb("FL", [128, 4, 128], FP16)
        tiny = sb("tiny", [128, 96], F32)
        st6, mv, ve, rs = tiny[:, 0:6], tiny[:, 6:8], tiny[:, 8:9], tiny[:, 9:10]
        mhalf, neg = tiny[:, 10:11], tiny[:, 11:12]
        nmx = [tiny[:, 12:16], tiny[:, 16:20]]
        rsum = [tiny[:, 20:24], tiny[:, 24:28]]
        rinv = [tiny[:, 28:32], tiny[:, 32:36]]
        idx = tiny[:, 36:52]
        amax, pw, gt, sc = tiny[:, 52:68], tiny[:, 68:84], nmx, tiny[:, 80:96]

        proj = pb("proj", [128, PROJ, 512])
        pS = pb("pS", [128, 512])
        pT = pb("pT", [128, 512])
        pV = pb("pV", [128, 2, 512])
        pO = pb("pO", [128, 512])

        P = Program()
        pe, act, dve, pool, sp = (Queue(sem("s_" + n)) for n in ("pe", "act", "dve", "pool", "sp"))
        names = {id(pe): "pe"}

        def add(queue, made, fn, *waits):
            if made is not None:
                P.done_by(queue, made)
            queue.add(made, fn, *waits)

        def dma(queue, name, dst, src, slot_sem, count, *waits):
            P.at[name] = (slot_sem, count)
            P.prod[(id(queue), len(queue.items))] = [name]
            queue.add(None, lambda e: (e.dma_start(dst, src).then_inc(slot_sem, 16), None)[1], *waits)

        s_eye, s_bias, s_pos = sem("s_eye"), sem("s_bias"), sem("s_pos")
        s_acc = [sem(f"s_acc{j}") for j in range(8)]
        s_out = [sem(f"s_out{j}") for j in range(8)]
        s_raw = [sem(f"s_raw{j}") for j in range(RAW)]
        s_cs = [sem(f"s_cs{j}") for j in range(RAW)]

        dma(sp, "POS", idx.bitcast(I32), pos, s_pos, 16)
        dma(sp, "X0", acc[:, 0, :], x[0], s_acc[0], 16)
        dma(sp, "EYE", ident[:, :], eye, s_eye, 16)
        for j in range(1, 4):
            dma(sp, f"X{j}", acc[:, j, :], x[j], s_acc[j], 16)

        add(dve, "MHALF", lambda e: e.memset(mhalf, -0.5))
        add(dve, "NEG", lambda e: e.memset(neg, -1.0e9))
        pf, pn = amax, pw
        add(dve, "IX1", lambda e: e.tensor_copy(pf, idx.bitcast(I32)), "POS")
        add(dve, "IX2", lambda e: e.tensor_scalar(pn, pf, 0.0, 512.0, ALU.is_lt, ALU.mult), "IX1")
        add(dve, "IX3", lambda e: e.tensor_tensor(pf, pf, pn, ALU.add), "IX2")
        add(dve, "IX4", lambda e: e.tensor_scalar(pn, pf, 0.0, 511.0, ALU.max, ALU.min), "IX3")
        add(dve, "IDX", lambda e: e.tensor_copy(idx.bitcast(U32), pn), "IX4")

        ring = {"n": 0, "free": [None] * RAW, "sem": [0] * RAW, "gather": [0] * RAW}

        def take(name, loads, *waits):
            place = ring["n"] % RAW
            ring["n"] += 1
            for i, (dst, src) in enumerate(loads(raw[:, place, :])):
                ring["sem"][place] += 16
                dma(sp, f"{name}.{i}" if i + 1 < len(loads(raw[:, place, :])) else name, dst, src,
                    s_raw[place], ring["sem"][place], ring["free"][place], *waits)
            return place

        def release(place, result):
            ring["free"][place] = result

        banks = {"n": 0, "free": [None] * PROJ}

        def bank():
            b = banks["n"] % PROJ
            banks["n"] += 1
            return b, banks["free"][b]

        def bank_free(b, result):
            banks["free"][b] = result

        t2_free = {"by": None}

        def split(name, hi, lo, src, view, free):
            place = take(name + ".raw", lambda r: [(view(r), src)])
            r = view(raw[:, place, :])
            add(act, name + ".hi", lambda e: e.copy(hi, r), name + ".raw", *free)
            add(pool, name, lambda e: e.tensor_tensor(lo, r, hi.bitcast(F32), ALU.subtract), name + ".hi")
            release(place, name)

        k4 = lambda r: r.rearrange("p (k d) -> p k d", k=4)

        def w_q(G, h):
            g = G % GROUPS
            split(f"WQ{G}.{h}", QH[:, h], QL[:, h], wq[4 * g + h], k4, [f"QP{4 * (2 * G - 1) + h}"] if G else [])

        def w_k(G):
            split(f"WK{G}", KH[:, :, :], KL[:, :, :], wk[G % GROUPS], k4, [f"KP{2 * G - 1}"] if G else [])

        def w_v(G):
            E = G - G % 2
            c = slice(128 * (G % 2), 128 * (G % 2) + 128)
            split(f"WV{G}", UH[:, :, c], UL[:, :, c], wv[G % GROUPS], k4, [f"VP{2 * E - 3}.3"] if E else [])

        def w_o(G, h):
            J = 4 * G + h
            r = J % WO_RING
            free = [f"OP{8 * ((J - WO_RING) // 4) + 7}"] if J >= WO_RING else []
            split(f"WO{G}.{h}", OH[:, r], OL[:, r], wo[4 * (G % GROUPS) + h], lambda v: v, free)

        def c_tile(s, t):
            T = 8 * (s // 16) + 4 * (s % 2) + t
            c = slice(512 * (s % 2) + 128 * t, 512 * (s % 2) + 128 * t + 128)
            free = [f"KP{s - 2}", f"VP{s - 4}.3"] if s >= 16 else []
            split(f"C{s}.{t}", CH[:, :, c], CL[:, :, c], ctxT[T], k4, free)

        def norm(tag, src, factor, *waits):
            add(dve, tag + ".st", lambda e: e.bn_stats(st6, src), *waits)
            add(dve, tag + ".mv", lambda e: e.bn_aggr(mv, st6), tag + ".st")
            add(dve, tag + ".ve", lambda e: e.tensor_scalar(ve, mv[:, 1:2], 1e-5, 1.0 / factor ** 2, ALU.add, ALU.mult),
                tag + ".mv")
            add(pool, tag + ".rs", lambda e: e.tensor_tensor(rs, ve, mhalf, ALU.pow), tag + ".ve", "MHALF")
            add(dve, tag + ".xn", lambda e: e.tensor_scalar(t2[:, :], src, mv[:, 0:1], rs, ALU.subtract, ALU.mult),
                tag + ".rs", t2_free["by"])

        def turn(tag, src, n, made_by):
            b, free = bank()

            def go(e):
                for k in range(n):
                    i = e.transpose(proj[:, b, 128 * k:128 * k + 128], src[:, 128 * k:128 * k + 128], ident[:, :])
                return i
            add(pe, tag, go, made_by, free, "EYE")
            return b, proj[:, b, 0:128 * n].rearrange("p (k t) -> p k t", k=n)

        def x_tile(s, t):
            j = 4 * (s % 2) + t
            T = 8 * (s // 16) + j
            if s < 16:
                src, here = acc[:, j, :], f"X{T}"
            else:
                place = take(f"XR{T}", lambda r: [(r, x[T])])
                src, here = raw[:, place, :], f"XR{T}"
            norm(f"LN{T}", src, 1.0, here)
            if s >= 16:
                release(place, f"LN{T}.xn")
            b, v = turn(f"XT{T}", t2, 4, f"LN{T}.xn")
            t2_free["by"] = f"XT{T}"
            c = slice(128 * j, 128 * j + 128)
            free = [f"QP{4 * (s - 2) + 3}"] if s >= 16 else []
            add(act, f"XH{T}", lambda e: e.copy(XH[:, :, c], v), f"XT{T}", *free)
            add(dve, f"XL{T}", lambda e: e.tensor_tensor(XL[:, :, c], v, XH[:, :, c].bitcast(F32), ALU.subtract),
                f"XH{T}")
            bank_free(b, f"XL{T}")

        def rope_tile(s, t):
            j = 4 * (s % 2) + t
            T = 8 * (s // 16) + j
            place = ring["n"] % RAW
            ring["n"] += 1
            ring["gather"][place] += 16
            P.at[f"CS{T}"] = (s_cs[place], ring["gather"][place])
            P.prod[(id(pool), len(pool.items))] = [f"CS{T}"]
            dst = raw[:, place, 0:256]
            pool.add(None, lambda e: (e.indirect_dma_start(
                out=dst, out_offset=None, in_=table,
                in_offset=bass.IndirectOffsetOnAxis(ap=idx[:, T:T + 1].bitcast(U32), axis=0)
            ).then_inc(s_cs[place], 16), None)[1], ring["free"][place], "IDX")
            b, v = turn(f"CT{T}", raw[:, place, :], 2, f"CS{T}")
            release(place, f"CT{T}")
            c = slice(128 * j, 128 * j + 128)
            free = [f"QR{4 * (s - 2) + 3}.t", f"KR{s - 2}.t"] if s >= 16 else []
            add(act, f"COS{T}", lambda e: e.copy(COS[:, c], v[:, 0, :]), f"CT{T}", *free)
            add(act, f"SIN{T}", lambda e: e.copy(SIN[:, c], v[:, 1, :]), f"CT{T}")
            bank_free(b, f"SIN{T}")

        def mask_pair(half, j):
            m = HALF * half + j
            p = 8 * half + j
            place = take(f"MR{m}", lambda r: [
                (r[64 * i:64 * i + 64, 0:128].rearrange("q (b k) -> q b k", b=2).bitcast(I32),
                 mask[2 * p:2 * p + 2].rearrange("b q k -> q b k")) for i in range(2)])
            free = [f"SM{m - 8}"] if half else []
            add(dve, f"MK{m}", lambda e: e.tensor_scalar(mk[:, j, :], raw[:, place, 0:128].bitcast(I32), 0.0, None,
                                                         ALU.is_equal), f"MR{m}", *free)
            release(place, f"MK{m}")

        def three(e, dst, left, right, first=True, last=True):
            n = len(left)
            for k in range(n):
                (lh, ll), (rh, rl) = left[k], right[k]
                e.matmul(dst, lh, rh, start=first and k == 0, stop=False)
                e.matmul(dst, lh, rl, start=False, stop=False)
                i = e.matmul(dst, ll, rh, start=False, stop=last and k == n - 1)
            return i

        def rotate(tag, b, dst, j0, free):
            c = slice(512 * j0, 512 * j0 + 512)
            src = proj[:, b, :]
            add(dve, tag + ".c", lambda e: e.tensor_tensor(
                dst, src.rearrange("p (a t) -> p a t", t=64), COS[:, c].rearrange("p (a t) -> p a t", t=64), ALU.mult),
                *free)
            add(dve, None, lambda e: e.tensor_tensor(t2[0:64, :], src[64:128], SIN[64:128, c], ALU.mult),
                t2_free["by"])
            add(dve, tag + ".t", lambda e: e.tensor_tensor(t2[64:128, :], src[0:64], SIN[0:64, c], ALU.mult))
            bank_free(b, tag + ".t")
            add(pool, tag, lambda e: e.tensor_tensor(
                dst, dst, t2[:, :].rearrange("p (a t) -> p a t", t=64), ALU.add), tag + ".c", tag + ".t")
            t2_free["by"] = tag

        def tiles(s):
            return [8 * (s // 16) + 4 * (s % 2) + t for t in range(4)]

        def project_q(n):
            s, h = n // 4, n % 4
            G = s // 2
            b, free = bank()
            c = slice(512 * (s % 2), 512 * (s % 2) + 512)
            waits = [f"WQ{G}.{h}", free] + ([f"XL{T}" for T in tiles(s)] if h == 0 and s % 16 < 2 else [])
            add(pe, f"QP{n}", lambda e: three(e, proj[:, b, :], [(QH[:, h, k], QL[:, h, k]) for k in range(4)],
                                              [(XH[:, k, c], XL[:, k, c]) for k in range(4)]), *waits)
            need = [f"QP{n}"] + ([f"QK{4 * (s - 2) + 3}"] if s >= 2 else [])
            need += [f"SIN{T}" for T in tiles(s)] if h == 0 and s % 16 < 2 else []
            rotate(f"QR{n}", b, qT[:, s % 2, :, h, :], s % 2, need)

        def project_k(s):
            G = s // 2
            b, free = bank()
            c = slice(512 * (s % 2), 512 * (s % 2) + 512)
            waits = [f"WK{G}", free] + ([f"C{s}.{t}" for t in range(4)] if s % 16 < 2 else [])
            add(pe, f"KP{s}", lambda e: three(e, proj[:, b, :], [(KH[:, k], KL[:, k]) for k in range(4)],
                                              [(CH[:, k, c], CL[:, k, c]) for k in range(4)]), *waits)
            need = [f"KP{s}"] + ([f"QK{4 * (s - 2) + 3}"] if s >= 2 else [])
            rotate(f"KR{s}", b, kT[:, s % 2, :].rearrange("p (a t) -> p a t", t=64), s % 2, need)

        def project_v(s, t):
            G = s // 2
            b, free = bank()
            j = 4 * (s % 2) + t
            c = slice(128 * j, 128 * j + 128)
            waits = [f"WV{G}", f"WV{G + 1}", f"C{s - s % 16 + s % 2}.{t}", free]
            add(pe, f"VP{s}.{t}", lambda e: three(e, proj[:, b, 0:256], [(CH[:, k, c], CL[:, k, c]) for k in range(4)],
                                                  [(UH[:, k, :], UL[:, k, :]) for k in range(4)]), *waits)
            add(act, f"VH{s}.{t}", lambda e: e.copy(VH[:, j, :], proj[:, b, 0:256]), f"VP{s}.{t}",
                *([f"PV{4 * (s - 2) + t}"] if s >= 2 else []))
            add(dve, f"VL{s}.{t}", lambda e: e.tensor_tensor(VL[:, j, :], proj[:, b, 0:256],
                                                             VH[:, j, :].bitcast(F32), ALU.subtract), f"VH{s}.{t}")
            bank_free(b, f"VL{s}.{t}")

        def scores(m):
            s, p = m // 4, m % 4

            def go(e):
                for hp in range(2):
                    for b in range(2):
                        i = e.matmul(pS[:, 128 * hp + 64 * b:128 * hp + 64 * b + 64],
                                     qT[:, s % 2, 2 * p + b, 2 * hp:2 * hp + 2, :].rearrange("p h t -> p (h t)"),
                                     kT[:, s % 2, 128 * p + 64 * b:128 * p + 64 * b + 64], start=True, stop=True)
                return i
            add(pe, f"QK{m}", go, f"QR{4 * s + 3}", f"KR{s}", f"SC{m - 1}" if m else None)
            v = sm[:, m % 2, :]
            add(act, f"SC{m}", lambda e: e.mul(v, pS[:, 0:256], SCALE), f"QK{m}", f"PT{m - 2}" if m >= 2 else None)

        def soft_max(m):
            v = sm[:, m % 2, :]
            v4 = v.rearrange("p (a k) -> p a k", a=4)
            i = m % 2
            j = m % 8
            add(dve, f"SM{m}", lambda e: e.copy_predicated(
                v.rearrange("p (h k) -> p h k", h=2), mk[:, j:j + 1, :].broadcast_to([128, 2, 128]),
                neg.unsqueeze(2).broadcast_to([128, 2, 128])), f"SC{m}", "NEG", f"MK{m - m % HALF + j}")
            add(dve, f"MX{m}", lambda e: e.tensor_reduce(nmx[i], v4, AX.X, ALU.max, negate=True), f"SM{m}")
            add(dve, f"SU{m}", lambda e: e.tensor_tensor(v4, v4, nmx[i].unsqueeze(2).broadcast_to([128, 4, 64]), ALU.add),
                f"MX{m}")

        def exponent(m):
            v = sm[:, m % 2, :]
            add(act, f"EX{m}", lambda e: e.activation(v, v, ACT.Exp), f"SU{m}")

        def divide(m):
            v4 = sm[:, m % 2, :].rearrange("p (a k) -> p a k", a=4)
            i = m % 2
            add(dve, f"RS{m}", lambda e: e.tensor_reduce(rsum[i], v4, AX.X, ALU.add), f"EX{m}")
            add(dve, f"RI{m}", lambda e: e.reciprocal(rinv[i], rsum[i]), f"RS{m}")
            add(dve, f"PN{m}", lambda e: e.tensor_tensor(v4, v4, rinv[i].unsqueeze(2).broadcast_to([128, 4, 64]),
                                                         ALU.mult), f"RI{m}")

        def turn_p(m):
            def go(e):
                for hp in range(2):
                    i = e.transpose(pT[:, 128 * hp:128 * hp + 128], sm[:, m % 2, 128 * hp:128 * hp + 128], ident[:, :])
                return i
            add(pe, f"PT{m}", go, f"PN{m}", f"PL{m - 1}" if m else None)

        def turned_p(m):
            add(act, f"PH{m}", lambda e: e.copy(PH[:, :], pT[:, 0:256]), f"PT{m}", f"PV{m - 1}" if m else None)

        def turned_pl(m):
            add(dve, f"PL{m}", lambda e: e.tensor_tensor(PL[:, :], pT[:, 0:256], PH[:, :].bitcast(F32), ALU.subtract),
                f"PH{m}")

        def values(m):
            s, p = m // 4, m % 4
            G = s // 2
            j = 4 * (s % 2) + p
            c = slice(128 * (G % 2), 128 * (G % 2) + 128)
            sv = s - 2 * (G % 2)

            def go(e):
                for n, (a, w) in enumerate(((VH, PH), (VH, PL), (VL, PH))):
                    for b in range(2):
                        r = slice(64 * b, 64 * b + 64)
                        i = e.matmul(pV[:, b, 0:256], a[r, j, c], w[r, :], start=n == 0, stop=n == 2)
                return i
            add(pe, f"PV{m}", go, f"PL{m}", f"VL{sv}.{p}", f"AL{m - 1}" if m else None)

        def attended(m):
            d = AH[:, m % 2].rearrange("p h (b t) -> p b h t", b=2)
            v = pV[:, :, 0:256].rearrange("p b (h t) -> p b h t", h=4)
            add(act, f"AH{m}", lambda e: e.copy(d, v), f"PV{m}", f"OP{m - 2}" if m >= 2 else None)

        def attended_l(m):
            d = AH[:, m % 2].rearrange("p h (b t) -> p b h t", b=2).bitcast(F32)
            o = AL[:, m % 2].rearrange("p h (b t) -> p b h t", b=2)
            v = pV[:, :, 0:256].rearrange("p b (h t) -> p b h t", h=4)
            add(dve, f"AL{m}", lambda e: e.tensor_tensor(o, v, d, ALU.subtract), f"AH{m}")

        def project_o(m):
            G = m // 8
            rs_ = [(4 * G + h) % WO_RING for h in range(4)]
            if m % 8 == 0:
                for h in range(4):
                    add(pe, f"OP{m}" if h == 3 else None, lambda e, h=h: three(
                        e, pO[:, :], [(AH[:, m % 2, h], AL[:, m % 2, h])], [(OH[:, rs_[h]], OL[:, rs_[h]])],
                        h == 0, h == 3), f"AL{m}", f"WO{G}.{h}", f"AC{m - 1}" if m else None)
            else:
                add(pe, f"OP{m}", lambda e: three(e, pO[:, :], [(AH[:, m % 2, h], AL[:, m % 2, h]) for h in range(4)],
                                                  [(OH[:, r], OL[:, r]) for r in rs_]), f"AL{m}", f"AC{m - 1}")

        def accumulate(m):
            j = m % 8
            T = 8 * (m // HALF) + j
            first = m % HALF < 8
            add(dve, f"AC{m}", lambda e: e.tensor_tensor(acc[:, j, :], pO[:, :], acc[:, j, :], ALU.add), f"OP{m}",
                (f"X{T}b" if T in (6, 7) else f"X{T}") if first else f"AC{m - 8}", f"LN{T}.xn" if first and T < 8 else None)

        def ffn_norm(m):
            j = m % 8
            norm(f"LF{m}", acc[:, j, :], 1024.0, f"AC{m}")
            b, v = turn(f"FT{m}", t2, 4, f"LF{m}.xn")
            t2_free["by"] = f"FT{m}"
            prev = m - 1 if m % 8 else m - HALF + 7
            add(act, f"FH{m}", lambda e: e.copy(FH[:, :, :], v), f"FT{m}", f"FM{prev}" if prev >= 56 else None)
            add(dve, f"FL{m}", lambda e: e.tensor_tensor(FL[:, :, :], v, FH[:, :, :], ALU.subtract), f"FH{m}")
            bank_free(b, f"FL{m}")

        def ffn(m):
            j = m % 8
            T = 8 * (m // HALF) + j
            b, free = bank()

            def go(e):
                for k in range(4):
                    e.matmul(proj[:, b, :], FH[:, k], W4[:, k], start=k == 0, stop=False)
                    i = e.matmul(proj[:, b, :], FL[:, k], W4[:, k], start=False, stop=k == 3)
                return i
            add(pe, f"FM{m}", go, f"FL{m}", free, *[f"W4.{i}" for i in range(4)])
            add(dve, f"FA{m}", lambda e: e.tensor_tensor(acc[:, j, :], proj[:, b, :], acc[:, j, :], ALU.add), f"FM{m}")
            bank_free(b, f"FA{m}")
            add(dve, f"FB{m}", lambda e: e.tensor_tensor(acc[:, j, :], acc[:, j, :], bias[:, :], ALU.add), f"FA{m}", "BIAS")
            dma(sp, f"OUT{T}", out[T], acc[:, j, :], s_out[j], 16 * (m // HALF + 1), f"FB{m}")

        A, B = acc[:, 6, :], acc[:, 7, :]
        last_quant = {"by": None}

        def quantise(i):
            place = take(f"FK{i}", lambda r: [(r, fkT[i])])
            w = raw[:, place, :]
            w3 = w.rearrange("p (b k) -> p b k", k=32)
            A3 = A.rearrange("p (b k) -> p b k", k=32)
            bc = lambda a: a.unsqueeze(2).broadcast_to([128, 16, 32])
            t = f"Q{i}."
            g16 = tiny[:, 12:28]
            seq = [
                lambda e: e.tensor_reduce(amax, w3, AX.X, ALU.max, apply_absolute_value=True),
                lambda e: e.tensor_scalar(amax, amax, 1e-30, None, ALU.max),
                lambda e: e.tensor_scalar(pw.bitcast(I32)[:, 0:16], amax.bitcast(I32), 0x7F800000, None, ALU.bitwise_and),
                lambda e: e.scalar_tensor_tensor(g16, pw, 1.5, amax, ALU.mult, ALU.is_lt),
                lambda e: e.tensor_scalar(g16, g16, 0.25, 0.25, ALU.mult, ALU.add),
                lambda e: e.tensor_tensor(pw, pw, g16, ALU.mult),
                lambda e: e.tensor_scalar(g16.bitcast(I32), pw.bitcast(I32), -1.0, float(0x7F000000), ALU.mult, ALU.add),
                lambda e: e.tensor_tensor(w3, w3, bc(g16), ALU.mult),
                lambda e: e.tensor_scalar(A.bitcast(I32), w.bitcast(I32), 0x7FFFFFFF, None, ALU.bitwise_and),
                lambda e: e.tensor_scalar(B, A, 5.0, 2.0, ALU.is_gt, ALU.mult),
                lambda e: e.scalar_tensor_tensor(B, A, 3.5, B, ALU.is_gt, ALU.add),
                lambda e: e.scalar_tensor_tensor(B, A, 2.5, B, ALU.is_gt, ALU.add),
                lambda e: e.tensor_scalar(B, B, 2.0, None, ALU.mult),
                lambda e: e.scalar_tensor_tensor(B, A, 1.75, B, ALU.is_gt, ALU.add),
                lambda e: e.scalar_tensor_tensor(B, A, 1.25, B, ALU.is_gt, ALU.add),
                lambda e: e.scalar_tensor_tensor(B, A, 0.75, B, ALU.is_gt, ALU.add),
                lambda e: e.scalar_tensor_tensor(B, A, 0.25, B, ALU.is_gt, ALU.add),
                lambda e: e.tensor_scalar(pw, pw, 0.5 / 1024.0, None, ALU.mult),
                lambda e: e.tensor_tensor(A3, B.rearrange("p (b k) -> p b k", k=32), bc(pw), ALU.mult),
                lambda e: e.scalar_tensor_tensor(B.bitcast(U32), w.bitcast(U32), 0x80000000, A.bitcast(U32),
                                                 ALU.bitwise_and, ALU.bitwise_or),
            ]
            for n, fn in enumerate(seq):
                add(dve, f"{t}{n}", fn, f"{t}{n - 1}" if n else f"FK{i}",
                    *((last_quant["by"], "LN6.xn", "LN7.xn") if n == 0 else ()))
            release(place, f"{t}{len(seq) - 1}")
            b, v = turn(t + "T", B, 4, f"{t}{len(seq) - 1}")
            add(act, f"W4.{i}", lambda e: e.copy(W4[:, :, 128 * i:128 * i + 128], v), t + "T")
            bank_free(b, f"W4.{i}")
            last_quant["by"] = t + "T"

        def load_x(half, j):
            T = 8 * half + j
            again = j in (6, 7)
            waits = [f"OUT{T - 8}"] if half else []
            dma(sp, f"X{T}", acc[:, j, :], x[T], s_acc[j], 16 * (half + 1 + (half and again)), *waits)

        def load_x_again(j):
            dma(sp, f"X{j}b", acc[:, j, :], x[j], s_acc[j], 32, last_quant["by"])

        jobs = {}

        def at(slot, *job):
            jobs.setdefault(max(slot, FIRST), []).append(job)

        for G in range(HALVES * GROUPS):
            for h in range(3):
                at(8 * G - 3 + h, w_q, G, h)
            at(8 * G - 1, w_k, G)
            at(8 * G + 1, w_q, G, 3)
            if G % 2 == 0:
                at(8 * G + 1, w_v, G)
                at(8 * G + 2, w_v, G + 1)
            at(8 * G + 3, w_o, G, 0)
            at(8 * G + 4, w_o, G, 1)
            at(8 * G + 8, w_o, G, 2)
            at(8 * G + 8, w_o, G, 3)
        for half in range(HALVES):
            s = 16 * half
            for t in range(4):
                at(4 * (s - 1) + t if half else (-2, -1, 0, 0)[t], c_tile, s, t)
                at(4 * s + t - (1 if half else 0) + (0 if half else 1), c_tile, s + 1, t)
            for j in range(8):
                at(4 * s + 1 + j if not half else 4 * s - 2 + j, mask_pair, half, j)

        end = PAIRS + 13
        for n in range(FIRST, end):
            m = n - 5
            if 0 <= n - 9 < PAIRS:
                accumulate(n - 9)
            if 0 <= n - 11 < PAIRS and (n - 11) % HALF >= 56:
                ffn(n - 11)
            if 0 <= n - 10 < PAIRS and (n - 10) % HALF >= 56:
                ffn_norm(n - 10)
            early = jobs.get(n, [])
            for job in [q for q in early if q[0] is w_o and q[2] >= 2]:
                job[0](*job[1:])
            if 0 <= n < PAIRS:
                project_q(n)
            if 0 <= m < PAIRS:
                scores(m)
                soft_max(m)
            if 0 <= m - 1 < PAIRS:
                turn_p(m - 1)
                turned_p(m - 1)
            if 0 <= m < PAIRS:
                exponent(m)
                divide(m)
            if 0 <= m - 2 < PAIRS:
                values(m - 2)
            if 0 <= m - 1 < PAIRS:
                turned_pl(m - 1)
            if 0 <= m - 2 < PAIRS:
                attended(m - 2)
                attended_l(m - 2)
            for job in [q for q in early if not (q[0] is w_o and q[2] >= 2)]:
                job[0](*job[1:])
            s = (n + 4) // 4
            if s % 16 < 2 and s < STEPS:
                x_tile(s, (n + 4) % 4)
                rope_tile(s, (n + 4) % 4)
            if 0 <= n < PAIRS and n % 4 == 1:
                project_k(n // 4)
            s, t = (n - 3) // 4, (n - 3) % 4
            if 0 <= s < STEPS and group_of(s) % 2 == 0:
                project_v(s, t)
            if 0 <= n - 8 < PAIRS:
                project_o(n - 8)
            if n == FIRST:
                for j in range(4, 8):
                    load_x(0, j)
                dma(sp, "BIAS", bias[:, :], fbias, s_bias, 16)
            if n in (3, 5, 7, 9):
                quantise((n - 3) // 2)
            if n == 10:
                load_x_again(6)
                load_x_again(7)
            if 62 <= n - 7 < 70:
                load_x(1, n - 7 - 62)

        for T in (8 * (HALVES - 1) + j for j in range(8)):
            sp.add(None, lambda e: None, f"OUT{T}")

        block = ctx.enter_context(nc.Block())

        @block.sync
        def _(eng):
            P.issue(sp, eng)

        @block.tensor
        def _(eng):
            P.issue(pe, eng)

        @block.scalar
        def _(eng):
            P.issue(act, eng)

        @block.vector
        def _(eng):
            P.issue(dve, eng)

        @block.gpsimd
        def _(eng):
            P.issue(pool, eng)


def rope_table():
    inv = (np.float32(1.0) / np.float32(10000.0) ** (np.arange(0, 128, 2, dtype=np.float32) / np.float32(128)))
    f = np.arange(512, dtype=np.float32)[:, None] * inv.astype(np.float32)[None, :]
    c, s = np.cos(f), np.sin(f)
    return np.ascontiguousarray(np.concatenate([c, c, s, -s], axis=1).astype(np.float32))


def kernel(x, ctx_4096, pos_BxS2, mask_BxSxS2_ik0, L0_xattn_Wq, L0_xattn_Wk, L0_xattn_Wv, L0_xattn_Wo,
           L0_ffn_kernel, L0_ffn_bias):
    import concourse.bacc as _bacc
    from concourse.bass_utils import run_bass_kernel_spmd as _run

    nc = _bacc.Bacc("TRN2", target_bir_lowering=False, num_devices=1)
    c = np.ascontiguousarray
    wide = lambda w: c(np.asarray(w).reshape(4, 128, -1, 128).transpose(2, 1, 0, 3))
    arrays = {
        "x": c(np.asarray(x).reshape(16, 128, 512)),
        "ctxT": c(np.asarray(ctx_4096).reshape(16, 128, 4, 128).transpose(0, 3, 2, 1)),
        "pos": c(np.asarray(pos_BxS2).reshape(16, 128).T),
        "mask": c(np.asarray(mask_BxSxS2_ik0)),
        "wq": wide(L0_xattn_Wq),
        "wk": wide(L0_xattn_Wk),
        "wv": wide(L0_xattn_Wv),
        "wo": c(np.asarray(L0_xattn_Wo).reshape(32, 128, 512)),
        "fkT": c(np.asarray(L0_ffn_kernel).T.reshape(4, 128, 512)),
        "fbias": c(np.broadcast_to(np.asarray(L0_ffn_bias)[None, :], (128, 512))),
        "table": rope_table(),
        "eye": np.eye(128, dtype=np.float32),
    }
    aps = [nc.dram_tensor(n, a.shape, mybir.dt.from_np(a.dtype), kind="ExternalInput").ap() for n, a in arrays.items()]
    out = nc.dram_tensor("out", (16, 128, 512), F32, kind="ExternalOutput").ap()
    build(nc, *aps, out)
    r = _run(nc, [arrays], core_ids=[0])
    return np.asarray(r.results[0]["out"]).reshape(32, 64, 512)
```

```python
from contextlib import ExitStack

import numpy as np

import concourse.bass as bass
from concourse import mybir

F32 = mybir.dt.float32
F32R = mybir.dt.float32r
BF16 = mybir.dt.bfloat16
FP16 = mybir.dt.float16
I32 = mybir.dt.int32
U32 = mybir.dt.uint32
U8 = mybir.dt.uint8
ALU = mybir.AluOpType
ACT = mybir.ActivationFunctionType
AX = mybir.AxisListType

HALVES = 2
GROUPS = 8
CHUNKS = 2
STEPS = HALVES * GROUPS * CHUNKS
PAIRS = 4 * STEPS
HALF = 8 * GROUPS
RAW = 4
WO_RING = 6
PROJ = 3
SCALE = float(1.0 / np.sqrt(np.float32(128.0)))
FIRST = -4


class Queue:

    def __init__(self, sem):
        self.sem, self.count, self.items = sem, 0, []

    def add(self, made, fn, *waits):
        self.items.append((fn, waits, made))


class Program:

    def __init__(self):
        self.at = {}
        self.prod = {}

    def done_by(self, queue, name):
        queue.count += 1
        assert name not in self.at, name
        self.at[name] = (queue.sem, queue.count)

    def issue(self, queue, eng):
        seen = {}
        for fn, waits, made in queue.items:
            for name in waits:
                if name is None:
                    continue
                sem, value = self.at[name]
                if seen.get(id(sem), 0) < value:
                    eng.wait_ge(sem, value)
                    seen[id(sem)] = value
            ins = fn(eng)
            if made is not None and ins is not None:
                ins.then_inc(queue.sem, 1)


def group_of(step):
    return (step // CHUNKS) % GROUPS


def build(nc, x, ctxT, pos, mask, wq, wk, wv, wo, fkT, fbias, table, eye, out):
    ctx = ExitStack()
    with ctx:
        def sb(name, shape, dt):
            return ctx.enter_context(nc.sbuf_tensor(name, shape, dt))

        def pb(name, shape):
            return ctx.enter_context(nc.psum_tensor(name, shape, F32))

        def sem(name):
            return ctx.enter_context(nc.semaphore(name))

        XH, XL = sb("XH", [128, 4, 1024], F32R), sb("XL", [128, 4, 1024], F32R)
        CH, CL = sb("CH", [128, 4, 1024], F32R), sb("CL", [128, 4, 1024], F32R)
        acc = sb("acc", [128, 8, 512], F32)
        COS, SIN = sb("COS", [128, 1024], F32), sb("SIN", [128, 1024], F32)
        qT = sb("qT", [128, 2, 8, 4, 64], F32)
        kT = sb("kT", [128, 2, 512], F32)
        VH, VL = sb("VH", [128, 8, 256], F32R), sb("VL", [128, 8, 256], F32R)
        QH, QL = sb("QH", [128, 4, 4, 128], F32R), sb("QL", [128, 4, 4, 128], F32R)
        KH, KL = sb("KH", [128, 4, 128], F32R), sb("KL", [128, 4, 128], F32R)
        UH, UL = sb("UH", [128, 4, 256], F32R), sb("UL", [128, 4, 256], F32R)
        OH, OL = sb("OH", [128, WO_RING, 512], F32R), sb("OL", [128, WO_RING, 512], F32R)
        raw = sb("raw", [128, RAW, 512], F32)
        AH, AL = sb("AH", [128, 2, 4, 128], F32R), sb("AL", [128, 2, 4, 128], F32R)
        t2 = sb("t2", [128, 512], F32)
        sm = sb("sm", [128, 2, 256], F32)
        PH, PL = sb("PH", [128, 256], F32R), sb("PL", [128, 256], F32R)
        ident = sb("ident", [128, 128], F32)
        mk = sb("mk", [128, 8, 128], U8)
        W4 = sb("W4", [128, 4, 512], BF16)
        bias = sb("bias", [128, 512], F32)
        FH, FL = sb("FH", [128, 4, 128], FP16), sb("FL", [128, 4, 128], FP16)
        tiny = sb("tiny", [128, 76], F32)
        st6, mv0, ve0, rs0 = tiny[:, 0:6], tiny[:, 6:8], tiny[:, 8:9], tiny[:, 9:10]
        mhalf, neg = tiny[:, 10:11], tiny[:, 11:12]
        nmx, rsum, rinv = tiny[:, 12:16], tiny[:, 16:20], tiny[:, 20:24]
        idx = tiny[:, 28:44]
        amax, pw = tiny[:, 44:60], tiny[:, 60:76]

        proj = pb("proj", [128, PROJ, 512])
        pS = pb("pS", [128, 512])
        pT = pb("pT", [128, 512])
        pV = pb("pV", [128, 2, 512])
        pO = pb("pO", [128, 512])

        P = Program()
        pe, act, dve, pool, sp = (Queue(sem("s_" + n)) for n in ("pe", "act", "dve", "pool", "sp"))
        names = {id(pe): "pe"}

        def add(queue, made, fn, *waits):
            if made is not None:
                P.done_by(queue, made)
            queue.add(made, fn, *waits)

        def dma(queue, name, dst, src, slot_sem, count, *waits):
            P.at[name] = (slot_sem, count)
            P.prod[(id(queue), len(queue.items))] = [name]
            queue.add(None, lambda e: (e.dma_start(dst, src).then_inc(slot_sem, 16), None)[1], *waits)

        s_eye, s_bias, s_pos = sem("s_eye"), sem("s_bias"), sem("s_pos")
        s_acc = [sem(f"s_acc{j}") for j in range(8)]
        s_out = [sem(f"s_out{j}") for j in range(8)]
        s_raw = [sem(f"s_raw{j}") for j in range(RAW)]
        s_cs = [sem(f"s_cs{j}") for j in range(8)]

        dma(sp, "POS", idx.bitcast(I32), pos, s_pos, 16)
        dma(sp, "X0", acc[:, 0, :], x[0], s_acc[0], 16)
        dma(sp, "EYE", ident[:, :], eye, s_eye, 16)
        for j in range(1, 4):
            dma(sp, f"X{j}", acc[:, j, :], x[j], s_acc[j], 16)

        add(dve, "MHALF", lambda e: e.memset(mhalf, -0.5))
        add(dve, "NEG", lambda e: e.memset(neg, -1.0e9))
        pf, pn = amax, pw
        add(dve, "IX1", lambda e: e.tensor_copy(pf, idx.bitcast(I32)), "POS")
        add(dve, "IX2", lambda e: e.tensor_scalar(pn, pf, 0.0, 512.0, ALU.is_lt, ALU.mult), "IX1")
        add(dve, "IX3", lambda e: e.tensor_tensor(pf, pf, pn, ALU.add), "IX2")
        add(dve, "IX4", lambda e: e.tensor_scalar(pn, pf, 0.0, 511.0, ALU.max, ALU.min), "IX3")
        add(dve, "IDX", lambda e: e.tensor_copy(idx.bitcast(U32), pn), "IX4")

        ring = {"n": 0, "free": [None] * RAW, "sem": [0] * RAW, "gather": [0] * 8}

        def hold(result=None):
            place = ring["n"] % RAW
            ring["n"] += 1
            free = ring["free"][place]
            assert free != "taken", "the ring comes round before the place is released"
            ring["free"][place] = result or "taken"
            return place, free

        def take(name, loads, result=None):
            place, free = hold(result)
            for i, (dst, src) in enumerate(loads(raw[:, place, :])):
                ring["sem"][place] += 16
                dma(sp, f"{name}.{i}" if i + 1 < len(loads(raw[:, place, :])) else name, dst, src,
                    s_raw[place], ring["sem"][place], free)
            return place

        def release(place, result):
            ring["free"][place] = result

        banks = {"n": 0, "free": [None] * PROJ}

        def bank():
            b = banks["n"] % PROJ
            banks["n"] += 1
            return b, banks["free"][b]

        def bank_free(b, result):
            banks["free"][b] = result

        t2_free = {"by": None}

        def split(name, hi, lo, src, view, free):
            place = take(name + ".raw", lambda r: [(view(r), src)])
            r = view(raw[:, place, :])
            add(act, name + ".hi", lambda e: e.copy(hi, r), name + ".raw", *free)
            add(pool, name, lambda e: e.tensor_tensor(lo, r, hi.bitcast(F32), ALU.subtract), name + ".hi")
            release(place, name)

        k4 = lambda r: r.rearrange("p (k d) -> p k d", k=4)

        def w_q(G, h):
            g = G % GROUPS
            split(f"WQ{G}.{h}", QH[:, h], QL[:, h], wq[4 * g + h], k4, [f"QP{4 * (2 * G - 1) + h}"] if G else [])

        def w_k(G):
            split(f"WK{G}", KH[:, :, :], KL[:, :, :], wk[G % GROUPS], k4, [f"KP{2 * G - 1}"] if G else [])

        def w_v(G):
            E = G - G % 2
            c = slice(128 * (G % 2), 128 * (G % 2) + 128)
            split(f"WV{G}", UH[:, :, c], UL[:, :, c], wv[G % GROUPS], k4, [f"VP{2 * E - 3}.3"] if E else [])

        def w_o(G, h):
            J = 4 * G + h
            r = J % WO_RING
            free = [f"OP{8 * ((J - WO_RING) // 4) + 7}"] if J >= WO_RING else []
            split(f"WO{G}.{h}", OH[:, r], OL[:, r], wo[4 * (G % GROUPS) + h], lambda v: v, free)

        def c_tile(s, t):
            T = 8 * (s // 16) + 4 * (s % 2) + t
            c = slice(512 * (s % 2) + 128 * t, 512 * (s % 2) + 128 * t + 128)
            free = [f"KP{s - 2}", f"VP{s - 4}.3"] if s >= 16 else []
            split(f"C{s}.{t}", CH[:, :, c], CL[:, :, c], ctxT[T], k4, free)

        def place_of(tag):
            if tag in ("LN0", "LN1", "LN2", "LN3"):
                T = int(tag[2:])
                return amax[:, 2 * T:2 * T + 2], amax[:, 8 + T:9 + T], amax[:, 12 + T:13 + T]
            return mv0, ve0, rs0

        def statistics(tag, src, factor, *waits):
            mv, ve, rs = place_of(tag)
            add(dve, tag + ".st", lambda e: e.bn_stats(st6, src), *waits)
            add(dve, tag + ".mv", lambda e: e.bn_aggr(mv, st6), tag + ".st")
            add(dve, tag + ".ve", lambda e: e.tensor_scalar(ve, mv[:, 1:2], 1e-5, 1.0 / factor ** 2, ALU.add, ALU.mult),
                tag + ".mv")
            add(pool, tag + ".rs", lambda e: e.tensor_tensor(rs, ve, mhalf, ALU.pow), tag + ".ve", "MHALF")

        def normalise(tag, dst, src, free):
            mv, ve, rs = place_of(tag)
            add(dve, tag + ".xn", lambda e: e.tensor_scalar(dst, src, mv[:, 0:1], rs, ALU.subtract, ALU.mult),
                tag + ".rs", free)

        def turn(tag, src, n, made_by):
            b, free = bank()

            def go(e):
                for k in range(n):
                    i = e.transpose(proj[:, b, 128 * k:128 * k + 128], src[:, 128 * k:128 * k + 128], ident[:, :])
                return i
            add(pe, tag, go, made_by, free, "EYE")
            return b, proj[:, b, 0:128 * n].rearrange("p (k t) -> p k t", k=n)

        def x_tile(s, t):
            j = 4 * (s % 2) + t
            T = 8 * (s // 16) + j
            if s < 16:
                src, here = acc[:, j, :], f"X{T}"
                place, free = hold(f"XT{T}")
            else:
                place, free = take(f"XR{T}", lambda r: [(r, x[T])], f"XT{T}"), None
                src, here = raw[:, place, :], f"XR{T}"
            dst = raw[:, place, :]
            statistics(f"LN{T}", src, 1.0, here)
            yield
            normalise(f"LN{T}", dst, src, free)
            yield
            b, v = turn(f"XT{T}", dst, 4, f"LN{T}.xn")
            c = slice(128 * j, 128 * j + 128)
            free = [f"QP{4 * (s - 2) + 3}"] if s >= 16 else []
            add(act, f"XH{T}", lambda e: e.copy(XH[:, :, c], v), f"XT{T}", *free)
            add(dve, f"XL{T}", lambda e: e.tensor_tensor(XL[:, :, c], v, XH[:, :, c].bitcast(F32), ALU.subtract),
                f"XH{T}")
            bank_free(b, f"XL{T}")
            yield

        def gather(T):
            if T < 8:
                place, free = T % RAW, None
                dst = qT[:, 1].rearrange("p a h t -> p (a h t)")[:, 256 * T:256 * T + 256]
            else:
                place, free = hold(f"CT{T}")
                dst = raw[:, place, 0:256]
            ring["gather"][T % 8] += 16
            s_g = s_cs[T % 8]
            P.at[f"CS{T}"] = (s_g, ring["gather"][T % 8])
            P.prod[(id(pool), len(pool.items))] = [f"CS{T}"]
            pool.add(None, lambda e: (e.indirect_dma_start(
                out=dst, out_offset=None, in_=table,
                in_offset=bass.IndirectOffsetOnAxis(ap=idx[:, T:T + 1].bitcast(U32), axis=0)
            ).then_inc(s_g, 16), None)[1], free, "IDX")
            gathered[T] = place, dst

        gathered = {}

        def rope_tile(s, t):
            j = 4 * (s % 2) + t
            T = 8 * (s // 16) + j
            place, src = gathered[T]
            b, v = turn(f"CT{T}", src, 2, f"CS{T}")
            c = slice(128 * j, 128 * j + 128)
            free = [f"QR{4 * (s - 2) + 3}.t", f"KR{s - 2}.t"] if s >= 16 else []
            add(act, f"COS{T}", lambda e: e.copy(COS[:, c], v[:, 0, :]), f"CT{T}", *free)
            add(act, f"SIN{T}", lambda e: e.copy(SIN[:, c], v[:, 1, :]), f"CT{T}")
            bank_free(b, f"SIN{T}")

        def mask_pair(half, j):
            m = HALF * half + j
            p = 8 * half + j
            place = take(f"MR{m}", lambda r: [
                (r[64 * i:64 * i + 64, 0:128].rearrange("q (b k) -> q b k", b=2).bitcast(I32),
                 mask[2 * p:2 * p + 2].rearrange("b q k -> q b k")) for i in range(2)])
            free = [f"SM{m - 8}"] if half else []
            add(dve, f"MK{m}", lambda e: e.tensor_scalar(mk[:, j, :], raw[:, place, 0:128].bitcast(I32), 0.0, None,
                                                         ALU.is_equal), f"MR{m}", *free)
            release(place, f"MK{m}")

        def three(e, dst, left, right, first=True, last=True):
            n = len(left)
            for k in range(n):
                (lh, ll), (rh, rl) = left[k], right[k]
                e.matmul(dst, lh, rh, start=first and k == 0, stop=False)
                e.matmul(dst, lh, rl, start=False, stop=False)
                i = e.matmul(dst, ll, rh, start=False, stop=last and k == n - 1)
            return i

        def rotate(tag, b, dst, j0, free):
            c = slice(512 * j0, 512 * j0 + 512)
            src = proj[:, b, :]
            add(dve, tag + ".c", lambda e: e.tensor_tensor(
                dst, src.rearrange("p (a t) -> p a t", t=64), COS[:, c].rearrange("p (a t) -> p a t", t=64), ALU.mult),
                *free)
            add(dve, None, lambda e: e.tensor_tensor(t2[0:64, :], src[64:128], SIN[64:128, c], ALU.mult),
                t2_free["by"])
            add(dve, tag + ".t", lambda e: e.tensor_tensor(t2[64:128, :], src[0:64], SIN[0:64, c], ALU.mult))
            bank_free(b, tag + ".t")
            add(pool, tag, lambda e: e.tensor_tensor(
                dst, dst, t2[:, :].rearrange("p (a t) -> p a t", t=64), ALU.add), tag + ".c", tag + ".t")
            t2_free["by"] = tag

        def tiles(s):
            return [8 * (s // 16) + 4 * (s % 2) + t for t in range(4)]

        def project_q(n):
            s, h = n // 4, n % 4
            G = s // 2
            b, free = bank()
            c = slice(512 * (s % 2), 512 * (s % 2) + 512)
            waits = [f"WQ{G}.{h}", free] + ([f"XL{T}" for T in tiles(s)] if h == 0 and s % 16 < 2 else [])
            add(pe, f"QP{n}", lambda e: three(e, proj[:, b, :], [(QH[:, h, k], QL[:, h, k]) for k in range(4)],
                                              [(XH[:, k, c], XL[:, k, c]) for k in range(4)]), *waits)
            need = [f"QP{n}"] + ([f"QK{4 * (s - 2) + 3}"] if s >= 2 else [])
            need += [f"SIN{T}" for T in tiles(s)] if h == 0 and s % 16 < 2 else []
            need += ["CT7"] if s == 1 else []
            rotate(f"QR{n}", b, qT[:, s % 2, :, h, :], s % 2, need)

        def project_k(s):
            G = s // 2
            b, free = bank()
            c = slice(512 * (s % 2), 512 * (s % 2) + 512)
            waits = [f"WK{G}", free] + ([f"C{s}.{t}" for t in range(4)] if s % 16 < 2 else [])
            add(pe, f"KP{s}", lambda e: three(e, proj[:, b, :], [(KH[:, k], KL[:, k]) for k in range(4)],
                                              [(CH[:, k, c], CL[:, k, c]) for k in range(4)]), *waits)
            need = [f"KP{s}"] + ([f"QK{4 * (s - 2) + 3}"] if s >= 2 else [])
            rotate(f"KR{s}", b, kT[:, s % 2, :].rearrange("p (a t) -> p a t", t=64), s % 2, need)

        def project_v(s, t):
            G = s // 2
            b, free = bank()
            j = 4 * (s % 2) + t
            c = slice(128 * j, 128 * j + 128)
            waits = [f"WV{G}", f"WV{G + 1}", f"C{s - s % 16 + s % 2}.{t}", free]
            add(pe, f"VP{s}.{t}", lambda e: three(e, proj[:, b, 0:256], [(CH[:, k, c], CL[:, k, c]) for k in range(4)],
                                                  [(UH[:, k, :], UL[:, k, :]) for k in range(4)]), *waits)
            add(act, f"VH{s}.{t}", lambda e: e.copy(VH[:, j, :], proj[:, b, 0:256]), f"VP{s}.{t}",
                *([f"PV{4 * (s - 2) + t}"] if s >= 2 else []))
            add(dve, f"VL{s}.{t}", lambda e: e.tensor_tensor(VL[:, j, :], proj[:, b, 0:256],
                                                             VH[:, j, :].bitcast(F32), ALU.subtract), f"VH{s}.{t}")
            bank_free(b, f"VL{s}.{t}")

        def scores(m):
            s, p = m // 4, m % 4

            def go(e):
                for hp in range(2):
                    for b in range(2):
                        i = e.matmul(pS[:, 128 * hp + 64 * b:128 * hp + 64 * b + 64],
                                     qT[:, s % 2, 2 * p + b, 2 * hp:2 * hp + 2, :].rearrange("p h t -> p (h t)"),
                                     kT[:, s % 2, 128 * p + 64 * b:128 * p + 64 * b + 64], start=True, stop=True)
                return i
            add(pe, f"QK{m}", go, f"QR{4 * s + 3}", f"KR{s}", f"SC{m - 1}" if m else None)
            v = sm[:, m % 2, :]
            add(act, f"SC{m}", lambda e: e.mul(v, pS[:, 0:256], SCALE), f"QK{m}", f"PT{m - 2}" if m >= 2 else None)

        def soft_max(m):
            v = sm[:, m % 2, :]
            v4 = v.rearrange("p (a k) -> p a k", a=4)
            j = m % 8
            add(dve, f"SM{m}", lambda e: e.copy_predicated(
                v.rearrange("p (h k) -> p h k", h=2), mk[:, j:j + 1, :].broadcast_to([128, 2, 128]),
                neg.unsqueeze(2).broadcast_to([128, 2, 128])), f"SC{m}", "NEG", f"MK{m - m % HALF + j}")
            add(dve, f"MX{m}", lambda e: e.tensor_reduce(nmx, v4, AX.X, ALU.max, negate=True), f"SM{m}")
            add(dve, f"SU{m}", lambda e: e.tensor_tensor(v4, v4, nmx.unsqueeze(2).broadcast_to([128, 4, 64]), ALU.add),
                f"MX{m}")

        def exponent(m):
            v = sm[:, m % 2, :]
            add(act, f"EX{m}", lambda e: e.activation(v, v, ACT.Exp), f"SU{m}")

        def divide(m):
            v4 = sm[:, m % 2, :].rearrange("p (a k) -> p a k", a=4)
            add(dve, f"RS{m}", lambda e: e.tensor_reduce(rsum, v4, AX.X, ALU.add), f"EX{m}")
            add(dve, f"RI{m}", lambda e: e.reciprocal(rinv, rsum), f"RS{m}")
            add(dve, f"PN{m}", lambda e: e.tensor_tensor(v4, v4, rinv.unsqueeze(2).broadcast_to([128, 4, 64]),
                                                         ALU.mult), f"RI{m}")

        def turn_p(m):
            def go(e):
                for hp in range(2):
                    i = e.transpose(pT[:, 128 * hp:128 * hp + 128], sm[:, m % 2, 128 * hp:128 * hp + 128], ident[:, :])
                return i
            add(pe, f"PT{m}", go, f"PN{m}", f"PL{m - 1}" if m else None)

        def turned_p(m):
            add(act, f"PH{m}", lambda e: e.copy(PH[:, :], pT[:, 0:256]), f"PT{m}", f"PV{m - 1}" if m else None)

        def turned_pl(m):
            add(dve, f"PL{m}", lambda e: e.tensor_tensor(PL[:, :], pT[:, 0:256], PH[:, :].bitcast(F32), ALU.subtract),
                f"PH{m}")

        def values(m):
            s, p = m // 4, m % 4
            G = s // 2
            j = 4 * (s % 2) + p
            c = slice(128 * (G % 2), 128 * (G % 2) + 128)
            sv = s - 2 * (G % 2)

            def go(e):
                for n, (a, w) in enumerate(((VH, PH), (VH, PL), (VL, PH))):
                    for b in range(2):
                        r = slice(64 * b, 64 * b + 64)
                        i = e.matmul(pV[:, b, 0:256], a[r, j, c], w[r, :], start=n == 0, stop=n == 2)
                return i
            add(pe, f"PV{m}", go, f"PL{m}", f"VL{sv}.{p}", f"AL{m - 1}" if m else None)

        def attended(m):
            d = AH[:, m % 2].rearrange("p h (b t) -> p b h t", b=2)
            v = pV[:, :, 0:256].rearrange("p b (h t) -> p b h t", h=4)
            add(act, f"AH{m}", lambda e: e.copy(d, v), f"PV{m}", f"OP{m - 2}" if m >= 2 else None)

        def attended_l(m):
            d = AH[:, m % 2].rearrange("p h (b t) -> p b h t", b=2).bitcast(F32)
            o = AL[:, m % 2].rearrange("p h (b t) -> p b h t", b=2)
            v = pV[:, :, 0:256].rearrange("p b (h t) -> p b h t", h=4)
            add(dve, f"AL{m}", lambda e: e.tensor_tensor(o, v, d, ALU.subtract), f"AH{m}")

        def project_o(m):
            G = m // 8
            rs_ = [(4 * G + h) % WO_RING for h in range(4)]
            if m % 8 == 0:
                for h in range(4):
                    add(pe, f"OP{m}" if h == 3 else None, lambda e, h=h: three(
                        e, pO[:, :], [(AH[:, m % 2, h], AL[:, m % 2, h])], [(OH[:, rs_[h]], OL[:, rs_[h]])],
                        h == 0, h == 3), f"AL{m}", f"WO{G}.{h}", f"AC{m - 1}" if m else None)
            else:
                add(pe, f"OP{m}", lambda e: three(e, pO[:, :], [(AH[:, m % 2, h], AL[:, m % 2, h]) for h in range(4)],
                                                  [(OH[:, r], OL[:, r]) for r in rs_]), f"AL{m}", f"AC{m - 1}")

        def accumulate(m):
            j = m % 8
            T = 8 * (m // HALF) + j
            first = m % HALF < 8
            add(dve, f"AC{m}", lambda e: e.tensor_tensor(acc[:, j, :], pO[:, :], acc[:, j, :], ALU.add), f"OP{m}",
                (f"X{T}b" if T in (6, 7) else f"X{T}") if first else f"AC{m - 8}", f"LN{T}.xn" if first and T < 8 else None)

        def ffn_tile(m):
            j = m % 8
            place, free = hold(f"FT{m}")
            dst = raw[:, place, :]
            statistics(f"LF{m}", acc[:, j, :], 1024.0, f"AC{m}")
            yield
            normalise(f"LF{m}", dst, acc[:, j, :], free)
            yield
            b, v = turn(f"FT{m}", dst, 4, f"LF{m}.xn")
            prev = m - 1 if m % 8 else m - HALF + 7
            add(act, f"FH{m}", lambda e: e.copy(FH[:, :, :], v), f"FT{m}", f"FM{prev}" if prev >= 56 else None)
            add(dve, f"FL{m}", lambda e: e.tensor_tensor(FL[:, :, :], v, FH[:, :, :], ALU.subtract), f"FH{m}")
            bank_free(b, f"FL{m}")
            yield

        def ffn(m):
            j = m % 8
            T = 8 * (m // HALF) + j
            b, free = bank()

            def go(e):
                for k in range(4):
                    e.matmul(proj[:, b, :], FH[:, k], W4[:, k], start=k == 0, stop=False)
                    i = e.matmul(proj[:, b, :], FL[:, k], W4[:, k], start=False, stop=k == 3)
                return i
            add(pe, f"FM{m}", go, f"FL{m}", free, *[f"W4.{i}" for i in range(4)])
            add(dve, f"FA{m}", lambda e: e.tensor_tensor(acc[:, j, :], proj[:, b, :], acc[:, j, :], ALU.add), f"FM{m}")
            bank_free(b, f"FA{m}")
            add(dve, f"FB{m}", lambda e: e.tensor_tensor(acc[:, j, :], acc[:, j, :], bias[:, :], ALU.add), f"FA{m}", "BIAS")
            dma(sp, f"OUT{T}", out[T], acc[:, j, :], s_out[j], 16 * (m // HALF + 1), f"FB{m}")

        A, B = acc[:, 6, :], acc[:, 7, :]
        last_quant = {"by": None}

        def quantise(i):
            place = take(f"FK{i}", lambda r: [(r, fkT[i])])
            w = raw[:, place, :]
            w3 = w.rearrange("p (b k) -> p b k", k=32)
            A3 = A.rearrange("p (b k) -> p b k", k=32)
            bc = lambda a: a.unsqueeze(2).broadcast_to([128, 16, 32])
            t = f"Q{i}."
            g16 = tiny[:, 12:28]
            seq = [
                lambda e: e.tensor_reduce(amax, w3, AX.X, ALU.max, apply_absolute_value=True),
                lambda e: e.tensor_scalar(amax, amax, 1e-30, None, ALU.max),
                lambda e: e.tensor_scalar(pw.bitcast(I32)[:, 0:16], amax.bitcast(I32), 0x7F800000, None, ALU.bitwise_and),
                lambda e: e.scalar_tensor_tensor(g16, pw, 1.5, amax, ALU.mult, ALU.is_lt),
                lambda e: e.tensor_scalar(g16, g16, 0.25, 0.25, ALU.mult, ALU.add),
                lambda e: e.tensor_tensor(pw, pw, g16, ALU.mult),
                lambda e: e.tensor_scalar(g16.bitcast(I32), pw.bitcast(I32), -1.0, float(0x7F000000), ALU.mult, ALU.add),
                lambda e: e.tensor_tensor(w3, w3, bc(g16), ALU.mult),
                lambda e: e.tensor_scalar(A.bitcast(I32), w.bitcast(I32), 0x7FFFFFFF, None, ALU.bitwise_and),
                lambda e: e.tensor_scalar(B, A, 5.0, 2.0, ALU.is_gt, ALU.mult),
                lambda e: e.scalar_tensor_tensor(B, A, 3.5, B, ALU.is_gt, ALU.add),
                lambda e: e.scalar_tensor_tensor(B, A, 2.5, B, ALU.is_gt, ALU.add),
                lambda e: e.tensor_scalar(B, B, 2.0, None, ALU.mult),
                lambda e: e.scalar_tensor_tensor(B, A, 1.75, B, ALU.is_gt, ALU.add),
                lambda e: e.scalar_tensor_tensor(B, A, 1.25, B, ALU.is_gt, ALU.add),
                lambda e: e.scalar_tensor_tensor(B, A, 0.75, B, ALU.is_gt, ALU.add),
                lambda e: e.scalar_tensor_tensor(B, A, 0.25, B, ALU.is_gt, ALU.add),
                lambda e: e.tensor_scalar(pw, pw, 0.5 / 1024.0, None, ALU.mult),
                lambda e: e.tensor_tensor(A3, B.rearrange("p (b k) -> p b k", k=32), bc(pw), ALU.mult),
                lambda e: e.scalar_tensor_tensor(B.bitcast(U32), w.bitcast(U32), 0x80000000, A.bitcast(U32),
                                                 ALU.bitwise_and, ALU.bitwise_or),
            ]
            for n, fn in enumerate(seq):
                add(dve, f"{t}{n}", fn, f"{t}{n - 1}" if n else f"FK{i}",
                    *((last_quant["by"], "LN6.xn", "LN7.xn") if n == 0 else ()))
            release(place, f"{t}{len(seq) - 1}")

        def quantised(i):
            t = f"Q{i}."
            b, v = turn(t + "T", B, 4, f"{t}19")
            add(act, f"W4.{i}", lambda e: e.copy(W4[:, :, 128 * i:128 * i + 128], v), t + "T")
            bank_free(b, f"W4.{i}")
            last_quant["by"] = t + "T"

        def load_x(half, j):
            T = 8 * half + j
            again = j in (6, 7)
            waits = [f"OUT{T - 8}"] if half else []
            dma(sp, f"X{T}", acc[:, j, :], x[T], s_acc[j], 16 * (half + 1 + (half and again)), *waits)

        def load_x_again(j):
            dma(sp, f"X{j}b", acc[:, j, :], x[j], s_acc[j], 32, last_quant["by"])

        jobs = {}

        def at(slot, *job):
            jobs.setdefault(max(slot, FIRST), []).append(job)

        for G in range(HALVES * GROUPS):
            for h in range(0 if G else 1, 3):
                at(8 * G - 3 + h, w_q, G, h)
            at(8 * G - 1, w_k, G)
            at(8 * G + 1, w_q, G, 3)
            if G % 2 == 0:
                at(8 * G + 1, w_v, G)
                at(8 * G + 2, w_v, G + 1)
            at(8 * G + 3, w_o, G, 0)
            at(8 * G + 4, w_o, G, 1)
            at(8 * G + 8, w_o, G, 2)
            at(8 * G + 8, w_o, G, 3)
        for half in range(HALVES):
            s = 16 * half
            for t in range(4):
                at(4 * (s - 1) + t if half else (-2, -1, 0, 0)[t], c_tile, s, t)
                at(4 * s + t - (1 if half else 0) + (0 if half else 1), c_tile, s + 1, t)
            for j in range(8):
                at(4 * s + 1 + j if not half else 4 * s - 2 + j, mask_pair, half, j)

        end = PAIRS + 13
        first = [x_tile(0, t) for t in range(4)]
        for t in range(4):
            gather(t)
            next(first[t])
        for t in range(4):
            next(first[t])
        for t in range(4):
            next(first[t])
            if t == 0:
                w_q(0, 0)
        gather(4)
        for t in range(4):
            rope_tile(0, t)

        for n in range(FIRST, end):
            m = n - 5
            if 0 <= n - 9 < PAIRS:
                accumulate(n - 9)
            staged = []
            if 0 <= n - 10 < PAIRS and (n - 10) % HALF >= 56:
                staged.append(ffn_tile(n - 10))
            s = (n + 4) // 4
            if s % 16 < 2 and 0 < s < STEPS:
                staged.append(x_tile(s, (n + 4) % 4))
            if len(staged) == 1:
                next(staged[0])
            early = jobs.get(n, [])
            for job in [q for q in early if q[0] is w_o and q[2] >= 2]:
                job[0](*job[1:])
            if 0 <= n < PAIRS:
                project_q(n)
            if 0 <= m < PAIRS:
                scores(m)
                soft_max(m)
            for i, tile in enumerate(staged):
                if len(staged) > 1:
                    next(tile)
                next(tile)
            if 0 <= m - 1 < PAIRS:
                turn_p(m - 1)
                turned_p(m - 1)
            if 0 <= m < PAIRS:
                exponent(m)
                divide(m)
            if 0 <= m - 2 < PAIRS:
                values(m - 2)
            if 0 <= m - 1 < PAIRS:
                turned_pl(m - 1)
            if 0 <= m - 2 < PAIRS:
                attended(m - 2)
                attended_l(m - 2)
            for job in [q for q in early if not (q[0] is w_o and q[2] >= 2)]:
                job[0](*job[1:])
            s = (n + 4) // 4
            if s % 16 < 2 and 0 < s < STEPS:
                rope_tile(s, (n + 4) % 4)
            s = (n + 5) // 4
            if s % 16 < 2 and 0 < s < STEPS and 8 * (s // 16) + 4 * (s % 2) + (n + 5) % 4 != 4:
                gather(8 * (s // 16) + 4 * (s % 2) + (n + 5) % 4)
            if 0 <= n < PAIRS and n % 4 == 1:
                project_k(n // 4)
            s, t = (n - 3) // 4, (n - 3) % 4
            if 0 <= s < STEPS and group_of(s) % 2 == 0:
                project_v(s, t)
            if 0 <= n - 11 < PAIRS and (n - 11) % HALF >= 56:
                ffn(n - 11)
            for tile in staged:
                next(tile)
            if n in (4, 6, 8, 10):
                quantised((n - 4) // 2)
            if 0 <= n - 8 < PAIRS:
                project_o(n - 8)
            if n == FIRST:
                for j in range(4, 8):
                    load_x(0, j)
                dma(sp, "BIAS", bias[:, :], fbias, s_bias, 16)
            if n in (3, 5, 7, 9):
                quantise((n - 3) // 2)
            if n == 10:
                load_x_again(6)
                load_x_again(7)
            if 62 <= n - 7 < 70:
                load_x(1, n - 7 - 62)

        for T in (8 * (HALVES - 1) + j for j in range(8)):
            sp.add(None, lambda e: None, f"OUT{T}")

        block = ctx.enter_context(nc.Block())

        @block.sync
        def _(eng):
            P.issue(sp, eng)

        @block.tensor
        def _(eng):
            P.issue(pe, eng)

        @block.scalar
        def _(eng):
            P.issue(act, eng)

        @block.vector
        def _(eng):
            P.issue(dve, eng)

        @block.gpsimd
        def _(eng):
            P.issue(pool, eng)


def rope_table():
    inv = (np.float32(1.0) / np.float32(10000.0) ** (np.arange(0, 128, 2, dtype=np.float32) / np.float32(128)))
    f = np.arange(512, dtype=np.float32)[:, None] * inv.astype(np.float32)[None, :]
    c, s = np.cos(f), np.sin(f)
    return np.ascontiguousarray(np.concatenate([c, c, s, -s], axis=1).astype(np.float32))


def kernel(x, ctx_4096, pos_BxS2, mask_BxSxS2_ik0, L0_xattn_Wq, L0_xattn_Wk, L0_xattn_Wv, L0_xattn_Wo,
           L0_ffn_kernel, L0_ffn_bias):
    import concourse.bacc as _bacc
    from concourse.bass_utils import run_bass_kernel_spmd as _run

    nc = _bacc.Bacc("TRN2", target_bir_lowering=False, num_devices=1)
    c = np.ascontiguousarray
    wide = lambda w: c(np.asarray(w).reshape(4, 128, -1, 128).transpose(2, 1, 0, 3))
    arrays = {
        "x": c(np.asarray(x).reshape(16, 128, 512)),
        "ctxT": c(np.asarray(ctx_4096).reshape(16, 128, 4, 128).transpose(0, 3, 2, 1)),
        "pos": c(np.asarray(pos_BxS2).reshape(16, 128).T),
        "mask": c(np.asarray(mask_BxSxS2_ik0)),
        "wq": wide(L0_xattn_Wq),
        "wk": wide(L0_xattn_Wk),
        "wv": wide(L0_xattn_Wv),
        "wo": c(np.asarray(L0_xattn_Wo).reshape(32, 128, 512)),
        "fkT": c(np.asarray(L0_ffn_kernel).T.reshape(4, 128, 512)),
        "fbias": c(np.broadcast_to(np.asarray(L0_ffn_bias)[None, :], (128, 512))),
        "table": rope_table(),
        "eye": np.eye(128, dtype=np.float32),
    }
    aps = [nc.dram_tensor(n, a.shape, mybir.dt.from_np(a.dtype), kind="ExternalInput").ap() for n, a in arrays.items()]
    out = nc.dram_tensor("out", (16, 128, 512), F32, kind="ExternalOutput").ap()
    build(nc, *aps, out)
    r = _run(nc, [arrays], core_ids=[0])
    return np.asarray(r.results[0]["out"]).reshape(32, 64, 512)
```

```python
from contextlib import ExitStack

import numpy as np

import concourse.bass as bass
from concourse import mybir

F32 = mybir.dt.float32
F32R = mybir.dt.float32r
BF16 = mybir.dt.bfloat16
FP16 = mybir.dt.float16
I32 = mybir.dt.int32
U32 = mybir.dt.uint32
U8 = mybir.dt.uint8
ALU = mybir.AluOpType
ACT = mybir.ActivationFunctionType
AX = mybir.AxisListType

HALVES = 2
GROUPS = 8
CHUNKS = 2
STEPS = HALVES * GROUPS * CHUNKS
PAIRS = 4 * STEPS
HALF = 8 * GROUPS
RAW = 4
WO_RING = 6
PROJ = 3
SCALE = float(1.0 / np.sqrt(np.float32(128.0)))
FIRST = -4


class Queue:

    def __init__(self, sem):
        self.sem, self.count, self.items = sem, 0, []

    def add(self, made, fn, *waits):
        self.items.append((fn, waits, made))


class Program:

    def __init__(self):
        self.at = {}

    def done_by(self, queue, name):
        queue.count += 1
        assert name not in self.at, name
        self.at[name] = (queue.sem, queue.count)

    def issue(self, queue, eng):
        seen = {}
        for fn, waits, made in queue.items:
            for name in waits:
                if name is None:
                    continue
                sem, value = self.at[name]
                if seen.get(id(sem), 0) < value:
                    eng.wait_ge(sem, value)
                    seen[id(sem)] = value
            ins = fn(eng)
            if made is not None and ins is not None:
                ins.then_inc(queue.sem, 1)


def group_of(step):
    return (step // CHUNKS) % GROUPS


def build(nc, x, ctxT, pos, mask, wq, wk, wv, wo, fkT, fbias, table, eye, out):
    ctx = ExitStack()
    with ctx:
        def sb(name, shape, dt):
            return ctx.enter_context(nc.sbuf_tensor(name, shape, dt))

        def pb(name, shape):
            return ctx.enter_context(nc.psum_tensor(name, shape, F32))

        def sem(name):
            return ctx.enter_context(nc.semaphore(name))

        XH, XL = sb("XH", [128, 4, 1024], F32R), sb("XL", [128, 4, 1024], F32R)
        CH, CL = sb("CH", [128, 4, 1024], F32R), sb("CL", [128, 4, 1024], F32R)
        acc = sb("acc", [128, 8, 512], F32)
        COS, SIN = sb("COS", [128, 1024], F32), sb("SIN", [128, 1024], F32)
        qT = sb("qT", [128, 2, 8, 4, 64], F32)
        kT = sb("kT", [128, 2, 512], F32)
        VS, PS = sb("VS", [128, 2, 8, 256], F32R), sb("PS", [128, 2, 256], F32R)
        ROWS = slice(0, 64), slice(64, 128)
        QH, QL = sb("QH", [128, 4, 4, 128], F32R), sb("QL", [128, 4, 4, 128], F32R)
        KH, KL = sb("KH", [128, 4, 128], F32R), sb("KL", [128, 4, 128], F32R)
        UH, UL = sb("UH", [128, 4, 256], F32R), sb("UL", [128, 4, 256], F32R)
        OH, OL = sb("OH", [128, WO_RING, 512], F32R), sb("OL", [128, WO_RING, 512], F32R)
        raw = sb("raw", [128, RAW, 512], F32)
        AH, AL = sb("AH", [128, 2, 4, 128], F32R), sb("AL", [128, 2, 4, 128], F32R)
        t2 = sb("t2", [128, 512], F32)
        PL = sb("PL", [128, 256], F32R)
        sm = sb("sm", [128, 2, 256], F32)
        ident = sb("ident", [128, 128], F32)
        mk = sb("mk", [128, 8, 128], U8)
        W4 = sb("W4", [128, 4, 512], BF16)
        F = sb("F", [128, 1024], FP16)
        FH, FL = (F[:, 512 * i:512 * i + 512].rearrange("p (k t) -> p k t", k=4) for i in range(2))
        tiny = sb("tiny", [128, 76], F32)
        st6, mv0, ve0, rs0 = tiny[:, 0:6], tiny[:, 6:8], tiny[:, 8:9], tiny[:, 9:10]
        mhalf, neg = tiny[:, 10:11], tiny[:, 11:12]
        nmx, rsum, rinv = tiny[:, 12:16], tiny[:, 16:20], tiny[:, 20:24]
        idx = tiny[:, 28:44]
        amax, pw = tiny[:, 44:60], tiny[:, 60:76]

        proj = pb("proj", [128, PROJ, 512])
        pS = pb("pS", [128, 512])
        pT = pb("pT", [128, 512])
        pV = pb("pV", [128, 2, 512])
        pO = pb("pO", [128, 512])

        P = Program()
        pe, act, dve, pool, sp = (Queue(sem("s_" + n)) for n in ("pe", "act", "dve", "pool", "sp"))

        def add(queue, made, fn, *waits):
            if made is not None:
                P.done_by(queue, made)
            queue.add(made, fn, *waits)

        def dma(queue, name, dst, src, slot_sem, count, *waits):
            P.at[name] = (slot_sem, count)
            queue.add(None, lambda e: (e.dma_start(dst, src).then_inc(slot_sem, 16), None)[1], *waits)

        s_fk = sem("s_fk")
        s_eye, s_pos = sem("s_eye"), sem("s_pos")
        s_acc = [sem(f"s_acc{j}") for j in range(8)]
        s_out = [sem(f"s_out{j}") for j in range(8)]
        s_raw = [sem(f"s_raw{j}") for j in range(RAW)]
        s_cs = [sem(f"s_cs{j}") for j in range(8)]

        dma(sp, "POS", idx.bitcast(I32), pos, s_pos, 16)
        dma(sp, "X0", acc[:, 0, :], x[0], s_acc[0], 16)
        dma(sp, "EYE", ident[:, :], eye, s_eye, 16)
        for j in range(1, 4):
            dma(sp, f"X{j}", acc[:, j, :], x[j], s_acc[j], 16)

        add(dve, "MHALF", lambda e: e.memset(mhalf, -0.5))
        add(dve, "NEG", lambda e: e.memset(neg, -1.0e9))
        pf, pn = amax, pw
        add(dve, "IX1", lambda e: e.tensor_copy(pf, idx.bitcast(I32)), "POS")
        add(dve, "IX2", lambda e: e.tensor_scalar(pn, pf, 0.0, 512.0, ALU.is_lt, ALU.mult), "IX1")
        add(dve, "IX3", lambda e: e.tensor_tensor(pf, pf, pn, ALU.add), "IX2")
        add(dve, "IX4", lambda e: e.tensor_scalar(pn, pf, 0.0, 511.0, ALU.max, ALU.min), "IX3")
        add(dve, "IDX", lambda e: e.tensor_copy(idx.bitcast(U32), pn), "IX4")

        ring = {"n": 0, "free": [None] * RAW, "sem": [0] * RAW, "gather": [0] * 8}

        def hold(result=None):
            place = ring["n"] % RAW
            ring["n"] += 1
            free = ring["free"][place]
            assert free != "taken", "the ring comes round before the place is released"
            ring["free"][place] = result or "taken"
            return place, free

        def take(name, loads, result=None):
            place, free = hold(result)
            for i, (dst, src) in enumerate(loads(raw[:, place, :])):
                ring["sem"][place] += 16
                dma(sp, f"{name}.{i}" if i + 1 < len(loads(raw[:, place, :])) else name, dst, src,
                    s_raw[place], ring["sem"][place], free)
            return place

        def release(place, result):
            ring["free"][place] = result

        banks = {"n": 0, "free": [None] * PROJ}

        def bank():
            b = banks["n"] % PROJ
            banks["n"] += 1
            return b, banks["free"][b]

        def bank_free(b, result):
            banks["free"][b] = result

        t2_free = {"by": None}
        scores_free = {"by": None}

        def split(name, hi, lo, src, view, free, on_dve=False):
            place = take(name + ".raw", lambda r: [(view(r), src)])
            r = view(raw[:, place, :])
            add(act, name + ".hi", lambda e: e.copy(hi, r), name + ".raw", *free)
            add(dve if on_dve else pool, name, lambda e: e.tensor_tensor(lo, r, hi.bitcast(F32), ALU.subtract),
                name + ".hi")
            release(place, name)

        k4 = lambda r: r.rearrange("p (k d) -> p k d", k=4)

        def w_q(G, h):
            g = G % GROUPS
            split(f"WQ{G}.{h}", QH[:, h], QL[:, h], wq[4 * g + h], k4, [f"QP{4 * (2 * G - 1) + h}"] if G else [])

        def w_k(G):
            split(f"WK{G}", KH[:, :, :], KL[:, :, :], wk[G % GROUPS], k4, [f"KP{2 * G - 1}"] if G else [])

        def w_v(G):
            E = G - G % 2
            c = slice(128 * (G % 2), 128 * (G % 2) + 128)
            split(f"WV{G}", UH[:, :, c], UL[:, :, c], wv[G % GROUPS], k4, [f"VP{2 * E - 3}.3"] if E else [], G < 2)

        def w_o(G, h):
            J = 4 * G + h
            r = J % WO_RING
            free = [f"OP{8 * ((J - WO_RING) // 4) + 7}"] if J >= WO_RING else []
            split(f"WO{G}.{h}", OH[:, r], OL[:, r], wo[4 * (G % GROUPS) + h], lambda v: v, free)

        def c_tile(s, t):
            T = 8 * (s // 16) + 4 * (s % 2) + t
            c = slice(512 * (s % 2) + 128 * t, 512 * (s % 2) + 128 * t + 128)
            free = [f"KP{s - 2}", f"VP{s - 4}.3"] if s >= 16 else []
            split(f"C{s}.{t}", CH[:, :, c], CL[:, :, c], ctxT[T], k4, free, s < 2)

        def place_of(tag):
            if tag in ("LN0", "LN1", "LN2", "LN3"):
                T = int(tag[2:])
                return amax[:, 2 * T:2 * T + 2], amax[:, 8 + T:9 + T], amax[:, 12 + T:13 + T]
            return mv0, ve0, rs0

        def statistics(tag, src, factor, *waits):
            mv, ve, rs = place_of(tag)
            add(dve, tag + ".st", lambda e: e.bn_stats(st6, src), *waits)
            add(dve, tag + ".mv", lambda e: e.bn_aggr(mv, st6), tag + ".st")
            add(dve, tag + ".ve", lambda e: e.tensor_scalar(ve, mv[:, 1:2], 1e-5, 1.0 / factor ** 2, ALU.add, ALU.mult),
                tag + ".mv")
            add(pool, tag + ".rs", lambda e: e.tensor_tensor(rs, ve, mhalf, ALU.pow), tag + ".ve", "MHALF")

        def normalise(tag, dst, src, free):
            mv, ve, rs = place_of(tag)
            add(dve, tag + ".xn", lambda e: e.tensor_scalar(dst, src, mv[:, 0:1], rs, ALU.subtract, ALU.mult),
                tag + ".rs", free)

        def turn(tag, src, n, made_by):
            b, free = bank()

            def go(e):
                for k in range(n):
                    i = e.transpose(proj[:, b, 128 * k:128 * k + 128], src[:, 128 * k:128 * k + 128], ident[:, :])
                return i
            add(pe, tag, go, made_by, free, "EYE")
            return b, proj[:, b, 0:128 * n].rearrange("p (k t) -> p k t", k=n)

        def x_tile(s, t):
            j = 4 * (s % 2) + t
            T = 8 * (s // 16) + j
            if s < 16:
                src, here = acc[:, j, :], f"X{T}"
                if T < 6:
                    dst, free = (qT[:, 0] if T < 4 else qT[:, 1]).rearrange("p a h t -> p (a h t)"), None
                    dst = dst[:, 512 * T:512 * T + 512] if T < 4 else dst[:, 512 * T - 1024:512 * T - 512]
                else:
                    place, free = hold(f"XT{T}")
                    dst = raw[:, place, :]
            else:
                place, free = take(f"XR{T}", lambda r: [(r, x[T])], f"XT{T}"), None
                src, here = raw[:, place, :], f"XR{T}"
                dst = raw[:, place, :]
            statistics(f"LN{T}", src, 1.0, here)
            yield
            normalise(f"LN{T}", dst, src, free)
            yield
            b, v = turn(f"XT{T}", dst, 4, f"LN{T}.xn")
            c = slice(128 * j, 128 * j + 128)
            free = [f"QP{4 * (s - 2) + 3}"] if s >= 16 else []
            add(act, f"XH{T}", lambda e: e.copy(XH[:, :, c], v), f"XT{T}", *free)
            add(dve, f"XL{T}", lambda e: e.tensor_tensor(XL[:, :, c], v, XH[:, :, c].bitcast(F32), ALU.subtract),
                f"XH{T}")
            bank_free(b, f"XL{T}")
            yield

        def gather(T):
            if T < 8:
                free = None
                dst = (sm[:, T] if T < 2 else t2[:, 256 * T - 512:256 * T - 256]) if T < 4 else (
                    qT[:, 1].rearrange("p a h t -> p (a h t)")[:, 256 * T - 1024:256 * T - 768])
            else:
                dst = F[:, 512 * (T % 2):512 * (T % 2) + 512].bitcast(F32)
                free = "Q7.T" if T < 10 else f"CT{T - 2}"
            ring["gather"][T % 8] += 16
            s_g = s_cs[T % 8]
            P.at[f"CS{T}"] = (s_g, ring["gather"][T % 8])
            pool.add(None, lambda e: (e.indirect_dma_start(
                out=dst, out_offset=None, in_=table,
                in_offset=bass.IndirectOffsetOnAxis(ap=idx[:, T:T + 1].bitcast(U32), axis=0)
            ).then_inc(s_g, 16), None)[1], free, "IDX")
            gathered[T] = dst

        gathered = {}

        def rope_tile(s, t):
            j = 4 * (s % 2) + t
            T = 8 * (s // 16) + j
            src = gathered[T]
            where = (pS, pT, pO, pV[:, 0])[T] if T < 4 else pS
            v = where[:, 256:512].rearrange("p (k t) -> p k t", k=2)

            def go(e):
                for k in range(2):
                    i = e.transpose(v[:, k], src[:, 128 * k:128 * k + 128], ident[:, :])
                return i
            add(pe, f"CT{T}", go, f"CS{T}", scores_free["by"] if T >= 4 else None, "EYE")
            c = slice(128 * j, 128 * j + 128)
            free = [f"QR{4 * (s - 2) + 3}.t", f"KR{s - 2}.t"] if s >= 16 else []
            add(act, f"COS{T}", lambda e: e.copy(COS[:, c], v[:, 0, :]), f"CT{T}", *free)
            add(act, f"SIN{T}", lambda e: e.copy(SIN[:, c], v[:, 1, :]), f"CT{T}")
            scores_free["by"] = f"SIN{T}"

        def mask_pair(half, j):
            m = HALF * half + j
            p = 8 * half + j
            place = take(f"MR{m}", lambda r: [
                (r[64 * i:64 * i + 64, 0:128].rearrange("q (b k) -> q b k", b=2).bitcast(I32),
                 mask[2 * p:2 * p + 2].rearrange("b q k -> q b k")) for i in range(2)])
            free = [f"SM{m - 8}"] if half else []
            add(dve, f"MK{m}", lambda e: e.tensor_scalar(mk[:, j, :], raw[:, place, 0:128].bitcast(I32), 0.0, None,
                                                         ALU.is_equal), f"MR{m}", *free)
            release(place, f"MK{m}")

        def three(e, dst, left, right, first=True, last=True):
            n = len(left)
            for k in range(n):
                (lh, ll), (rh, rl) = left[k], right[k]
                e.matmul(dst, lh, rh, start=first and k == 0, stop=False)
                e.matmul(dst, lh, rl, start=False, stop=False)
                i = e.matmul(dst, ll, rh, start=False, stop=last and k == n - 1)
            return i

        def rotate(tag, b, dst, j0, free):
            c = slice(512 * j0, 512 * j0 + 512)
            src = proj[:, b, :]
            add(dve, tag + ".c", lambda e: e.tensor_tensor(
                dst, src.rearrange("p (a t) -> p a t", t=64), COS[:, c].rearrange("p (a t) -> p a t", t=64), ALU.mult),
                *free)
            add(dve, None, lambda e: e.tensor_tensor(t2[0:64, :], src[64:128], SIN[64:128, c], ALU.mult),
                t2_free["by"])
            add(dve, tag + ".t", lambda e: e.tensor_tensor(t2[64:128, :], src[0:64], SIN[0:64, c], ALU.mult))
            bank_free(b, tag + ".t")
            add(pool, tag, lambda e: e.tensor_tensor(
                dst, dst, t2[:, :].rearrange("p (a t) -> p a t", t=64), ALU.add), tag + ".c", tag + ".t")
            t2_free["by"] = tag

        def tiles(s):
            return [8 * (s // 16) + 4 * (s % 2) + t for t in range(4)]

        def project_q(n):
            s, h = n // 4, n % 4
            G = s // 2
            b, free = bank()
            c = slice(512 * (s % 2), 512 * (s % 2) + 512)
            waits = [f"WQ{G}.{h}", free] + ([f"XL{T}" for T in tiles(s)] if h == 0 and s % 16 < 2 else [])
            add(pe, f"QP{n}", lambda e: three(e, proj[:, b, :], [(QH[:, h, k], QL[:, h, k]) for k in range(4)],
                                              [(XH[:, k, c], XL[:, k, c]) for k in range(4)]), *waits)
            need = [f"QP{n}"] + ([f"QK{4 * (s - 2) + 3}"] if s >= 2 else [])
            need += [f"SIN{T}" for T in tiles(s)] if h == 0 and s % 16 < 2 else []
            need += ["CT7", "XT5"] if s == 1 else ["XT3", "CT3"] if s == 0 else []
            rotate(f"QR{n}", b, qT[:, s % 2, :, h, :], s % 2, need)

        def project_k(s):
            G = s // 2
            b, free = bank()
            c = slice(512 * (s % 2), 512 * (s % 2) + 512)
            waits = [f"WK{G}", free] + ([f"C{s}.{t}" for t in range(4)] if s % 16 < 2 else [])
            add(pe, f"KP{s}", lambda e: three(e, proj[:, b, :], [(KH[:, k], KL[:, k]) for k in range(4)],
                                              [(CH[:, k, c], CL[:, k, c]) for k in range(4)]), *waits)
            need = [f"KP{s}"] + ([f"QK{4 * (s - 2) + 3}"] if s >= 2 else [])
            rotate(f"KR{s}", b, kT[:, s % 2, :].rearrange("p (a t) -> p a t", t=64), s % 2, need)

        def project_v(s, t):
            G = s // 2
            b, free = bank()
            j = 4 * (s % 2) + t
            c = slice(128 * j, 128 * j + 128)
            waits = [f"WV{G}", f"WV{G + 1}", f"C{s - s % 16 + s % 2}.{t}", free]
            add(pe, f"VP{s}.{t}", lambda e: three(e, proj[:, b, 0:256], [(CH[:, k, c], CL[:, k, c]) for k in range(4)],
                                                  [(UH[:, k, :], UL[:, k, :]) for k in range(4)]), *waits)
            free = [f"PV{4 * (s - 2) + t}"] if s >= 2 else []
            for i in range(2):
                add(act, f"VH{s}.{t}.{i}", lambda e, i=i: e.copy(VS[ROWS[i], i, j, :], proj[ROWS[i], b, 0:256]),
                    f"VP{s}.{t}", *free)
            for i in range(2):
                add(dve, f"VL{s}.{t}" if i else None, lambda e, i=i: e.tensor_tensor(
                    VS[ROWS[1 - i], i, j, :], proj[ROWS[i], b, 0:256], VS[ROWS[i], i, j, :].bitcast(F32),
                    ALU.subtract), f"VH{s}.{t}.{i}")
            bank_free(b, f"VL{s}.{t}")

        def scores(m):
            s, p = m // 4, m % 4

            def go(e):
                for hp in range(2):
                    for b in range(2):
                        i = e.matmul(pS[:, 128 * hp + 64 * b:128 * hp + 64 * b + 64],
                                     qT[:, s % 2, 2 * p + b, 2 * hp:2 * hp + 2, :].rearrange("p h t -> p (h t)"),
                                     kT[:, s % 2, 128 * p + 64 * b:128 * p + 64 * b + 64], start=True, stop=True)
                return i
            add(pe, f"QK{m}", go, f"QR{4 * s + 3}", f"KR{s}", scores_free["by"])
            scores_free["by"] = f"SC{m}"
            v = sm[:, m % 2, :]
            add(act, f"SC{m}", lambda e: e.mul(v, pS[:, 0:256], SCALE), f"QK{m}", f"PT{m - 2}" if m >= 2 else None)

        def soft_max(m):
            v = sm[:, m % 2, :]
            v4 = v.rearrange("p (a k) -> p a k", a=4)
            j = m % 8
            add(dve, f"SM{m}", lambda e: e.copy_predicated(
                v.rearrange("p (h k) -> p h k", h=2), mk[:, j:j + 1, :].broadcast_to([128, 2, 128]),
                neg.unsqueeze(2).broadcast_to([128, 2, 128])), f"SC{m}", "NEG", f"MK{m - m % HALF + j}")
            add(dve, f"MX{m}", lambda e: e.tensor_reduce(nmx, v4, AX.X, ALU.max, negate=True), f"SM{m}")

        def exponent(m):
            v4 = sm[:, m % 2, :].rearrange("p (a k) -> p a k", a=4)
            for a in range(4):
                add(act, f"EX{m}" if a == 3 else None, lambda e, a=a: e.activation(
                    v4[:, a], v4[:, a], ACT.Exp, bias=nmx[:, a:a + 1], accum_out=rsum[:, a:a + 1]), f"MX{m}",
                    f"RI{m - 1}" if m else None)

        def divide(m):
            v4 = sm[:, m % 2, :].rearrange("p (a k) -> p a k", a=4)
            add(dve, f"RI{m}", lambda e: e.reciprocal(rinv, rsum), f"EX{m}")
            add(dve, f"PN{m}", lambda e: e.tensor_tensor(v4, v4, rinv.unsqueeze(2).broadcast_to([128, 4, 64]),
                                                         ALU.mult), f"RI{m}")

        def turn_p(m):
            def go(e):
                for hp in range(2):
                    i = e.transpose(pT[:, 128 * hp:128 * hp + 128], sm[:, m % 2, 128 * hp:128 * hp + 128], ident[:, :])
                return i
            add(pe, f"PT{m}", go, f"PN{m}", *([f"PL{m - 1}", f"PX{m - 1}"] if m else []))

        def turned_p(m):
            for i in range(2):
                add(act, f"PH{m}.{i}", lambda e, i=i: e.copy(PS[ROWS[i], i, :], pT[ROWS[i], 0:256]), f"PT{m}",
                    f"PV{m - 1}" if m else None)

        def turned_px(m):
            for i in range(2):
                add(act, f"PX{m}" if i else None, lambda e, i=i: e.copy(
                    PS[ROWS[1 - i], i, :], PS[ROWS[i], i, :].bitcast(F32)), f"PH{m}.{i}")

        def turned_pl(m):
            for i in range(2):
                add(dve, f"PL{m}" if i else None, lambda e, i=i: e.tensor_tensor(
                    PL[ROWS[i], :], pT[ROWS[i], 0:256], PS[ROWS[i], i, :].bitcast(F32),
                    ALU.subtract), f"PH{m}.{i}")

        def values(m):
            s, p = m // 4, m % 4
            G = s // 2
            j = 4 * (s % 2) + p
            c = slice(128 * (G % 2), 128 * (G % 2) + 128)
            sv = s - 2 * (G % 2)

            def go(e):
                for b in range(2):
                    r = ROWS[b]
                    e.matmul(pV[:, b, 0:256], VS[:, b, j, c], PS[:, b, :], start=True, stop=False)
                    i = e.matmul(pV[:, b, 0:256], VS[r, b, j, c], PL[r, :], start=False, stop=True)
                return i
            add(pe, f"PV{m}", go, f"PL{m}", f"PX{m}", f"VL{sv}.{p}", f"AL{m - 1}" if m else None)

        def attended(m):
            d = AH[:, m % 2].rearrange("p h (b t) -> p b h t", b=2)
            v = pV[:, :, 0:256].rearrange("p b (h t) -> p b h t", h=4)
            add(act, f"AH{m}", lambda e: e.copy(d, v), f"PV{m}", f"OP{m - 2}" if m >= 2 else None)

        def attended_l(m):
            d = AH[:, m % 2].rearrange("p h (b t) -> p b h t", b=2).bitcast(F32)
            o = AL[:, m % 2].rearrange("p h (b t) -> p b h t", b=2)
            v = pV[:, :, 0:256].rearrange("p b (h t) -> p b h t", h=4)
            add(dve, f"AL{m}", lambda e: e.tensor_tensor(o, v, d, ALU.subtract), f"AH{m}")

        def project_o(m):
            G = m // 8
            rs_ = [(4 * G + h) % WO_RING for h in range(4)]
            if m % 8 == 0:
                def high(e, h):
                    for a in (AH, AL):
                        e.matmul(pO[:, :], a[:, m % 2, h], OH[:, rs_[h]], start=h == 0 and a is AH, stop=False)

                def low(e, h):
                    return e.matmul(pO[:, :], AH[:, m % 2, h], OL[:, rs_[h]], start=False, stop=h == 3)
                for h in range(4):
                    add(pe, None, lambda e, h=h: high(e, h), f"AL{m}", f"WO{G}.{h}.hi", f"AC{m - 1}" if m else None)
                for h in range(4):
                    add(pe, f"OP{m}" if h == 3 else None, lambda e, h=h: low(e, h), f"WO{G}.{h}")
            else:
                add(pe, f"OP{m}", lambda e: three(e, pO[:, :], [(AH[:, m % 2, h], AL[:, m % 2, h]) for h in range(4)],
                                                  [(OH[:, r], OL[:, r]) for r in rs_]), f"AL{m}", f"AC{m - 1}")

        def accumulate(m):
            j = m % 8
            T = 8 * (m // HALF) + j
            first = m % HALF < 8
            add(dve, f"AC{m}", lambda e: e.tensor_tensor(acc[:, j, :], pO[:, :], acc[:, j, :], ALU.add), f"OP{m}",
                f"X{T}" if first else f"AC{m - 8}", f"LN{T}.xn" if first and T < 8 else None)

        def ffn_tile(m):
            j = m % 8
            here, free = hold(f"FT{m}")
            dst = raw[:, here, :]
            statistics(f"LF{m}", acc[:, j, :], 1024.0, f"AC{m}")
            yield
            normalise(f"LF{m}", dst, acc[:, j, :], free)
            place = take(f"FC{m}", lambda r: [(r, fbias)])
            add(pool, f"FB{m}", lambda e: e.tensor_tensor(acc[:, j, :], acc[:, j, :], raw[:, place, :], ALU.add),
                f"LF{m}.xn", f"FC{m}")
            release(place, f"FB{m}")
            yield
            b, v = turn(f"FT{m}", dst, 4, f"LF{m}.xn")
            prev = m - 1 if m % 8 else m - HALF + 7
            add(act, f"FH{m}", lambda e: e.copy(FH[:, :, :], v), f"FT{m}", f"FM{prev}" if prev >= 56 else "CT15")
            add(dve, f"FL{m}", lambda e: e.tensor_tensor(FL[:, :, :], v, FH[:, :, :], ALU.subtract), f"FH{m}")
            bank_free(b, f"FL{m}")
            yield

        def ffn(m):
            j = m % 8
            T = 8 * (m // HALF) + j
            b, free = bank()

            def go(e):
                for k in range(4):
                    e.matmul(proj[:, b, :], FH[:, k], W4[:, k], start=k == 0, stop=False)
                    i = e.matmul(proj[:, b, :], FL[:, k], W4[:, k], start=False, stop=k == 3)
                return i
            add(pe, f"FM{m}", go, f"FL{m}", free, *[f"W4.{i}" for i in range(8)])
            bank_free(b, f"FA{m}")
            add(dve, f"FA{m}", lambda e: e.tensor_tensor(acc[:, j, :], proj[:, b, :], acc[:, j, :], ALU.add), f"FM{m}", f"FB{m}")
            dma(sp, f"OUT{T}", out[T], acc[:, j, :], s_out[j], 16 * (m // HALF + 1), f"FA{m}")

        A, B = (F[:, 512 * i:512 * i + 512].bitcast(F32) for i in range(2))
        last_quant = {"by": None, "load": None}

        def quantise(i):
            b3 = lambda a: a.rearrange("p (b k) -> p b k", k=32)
            A3, B3, AI = b3(A), b3(B), A.bitcast(I32)
            bc = lambda a: a.unsqueeze(2).broadcast_to([128, 8, 32])
            t = f"Q{i}."
            src, c = fkT[i // 2][:, 256 * (i % 2):256 * (i % 2) + 256], slice(128 * (i // 2), 128 * (i // 2) + 128)
            g, p = amax[:, 0:8], pw[:, 0:8]
            pi, gi = p.bitcast(I32), g.bitcast(I32)
            steps = [
                lambda e: e.tensor_reduce(g, A3, AX.X, ALU.max, apply_absolute_value=True),
                lambda e: e.tensor_scalar(g, g, 1e-30, None, ALU.max),
                lambda e: e.tensor_scalar(pi, gi, 0x7F800000, None, ALU.bitwise_and),
                lambda e: e.scalar_tensor_tensor(g, p, 1.5, g, ALU.mult, ALU.is_lt),
                lambda e: e.tensor_scalar(g, g, 0.25, 0.25, ALU.mult, ALU.add),
                lambda e: e.tensor_tensor(p, p, g, ALU.mult),
                lambda e: e.tensor_scalar(gi, pi, -1.0, float(0x7F000000), ALU.mult, ALU.add),
                lambda e: e.tensor_tensor(A3, A3, bc(g), ALU.mult),
                lambda e: e.tensor_scalar(AI, AI, 0x7FFFFFFF, None, ALU.bitwise_and),
                lambda e: e.tensor_scalar(B, A, 5.0, 2.0, ALU.is_gt, ALU.mult),
                lambda e: e.scalar_tensor_tensor(B, A, 3.5, B, ALU.is_gt, ALU.add),
                lambda e: e.scalar_tensor_tensor(B, A, 2.5, B, ALU.is_gt, ALU.add),
                lambda e: e.tensor_scalar(B, B, 2.0, None, ALU.mult),
                lambda e: e.scalar_tensor_tensor(B, A, 1.75, B, ALU.is_gt, ALU.add),
                lambda e: e.scalar_tensor_tensor(B, A, 1.25, B, ALU.is_gt, ALU.add),
                lambda e: e.scalar_tensor_tensor(B, A, 0.75, B, ALU.is_gt, ALU.add),
                lambda e: e.scalar_tensor_tensor(B, A, 0.25, B, ALU.is_gt, ALU.add),
                lambda e: e.tensor_scalar(p, p, 0.5 / 1024.0, None, ALU.mult),
                lambda e: e.tensor_tensor(A3, B3, bc(p), ALU.mult),
            ]
            dma(sp, f"FK{i}", A, src, s_fk, 16 * (i + 1), last_quant["load"])
            for n, fn in enumerate(steps):
                add(dve, f"{t}{n}", fn, f"{t}{n - 1}" if n else f"FK{i}", last_quant["by"] if n == 9 else None)
                if n > 7 or n in (0, 4):
                    yield
            place = take(f"FS{i}", lambda r: [(r[:, 0:256], src)])
            add(dve, t + "B", lambda e: e.scalar_tensor_tensor(
                B.bitcast(U32), raw[:, place, 0:256].bitcast(U32), 0x80000000, A.bitcast(U32),
                ALU.bitwise_and, ALU.bitwise_or), f"{t}18", f"FS{i}")
            release(place, t + "B")
            last_quant["load"] = t + "B"
            yield
            yield
            yield
            b, v = turn(t + "T", B, 2, t + "B")
            add(act, f"W4.{i}", lambda e: e.copy(W4[:, 2 * (i % 2):2 * (i % 2) + 2, c], v), t + "T")
            bank_free(b, f"W4.{i}")
            last_quant["by"] = t + "T"
            yield

        def load_x(half, j):
            T = 8 * half + j
            waits = [f"OUT{T - 8}"] if half else []
            dma(sp, f"X{T}", acc[:, j, :], x[T], s_acc[j], 16 * (half + 1), *waits)

        jobs = {}

        def at(slot, *job):
            jobs.setdefault(max(slot, FIRST), []).append(job)

        for G in range(HALVES * GROUPS):
            for h in range(0 if G else 1, 3):
                at(8 * G - 3 + h, w_q, G, h)
            at(8 * G - 2, w_k, G)
            at(8 * G + 1, w_q, G, 3)
            if G % 2 == 0:
                at(8 * G, w_v, G)
                at(8 * G + 2, w_v, G + 1)
            at(8 * G + 3, w_o, G, 0)
            at(8 * G + 4, w_o, G, 1)
            at(8 * G + 8, w_o, G, 2)
            at(8 * G + 8, w_o, G, 3)
        for half in range(HALVES):
            s = 16 * half
            for t in range(4):
                at(4 * (s - 1) + t if half else (-2, -1, 0, 0)[t], c_tile, s, t)
                at(4 * s + t + (0 if half else 1), c_tile, s + 1, t)
            for j in range(8):
                at(4 * s + 1 + j if not half else 4 * s - 2 + j, mask_pair, half, j)

        end = PAIRS + 13
        x_slots = {-2: 4, -1: 5, 0: 6, 1: 7}
        x_slots.update({HALF - 4 + t: 8 + t for t in range(8)})
        weights = (None for i in range(8) for _ in quantise(i))
        rope_slots = {t: 4 + t for t in range(4)}
        rope_slots.update({HALF - 4 + t: 8 + t for t in range(8)})
        ffn_slots = {HALF + 4 + t: HALF - 8 + t for t in range(8)}
        ffn_slots.update({PAIRS + 2 + t: PAIRS - 8 + t for t in range(8)})

        def turn_rope(T):
            rope_tile(16 * (T // 8) + T % 8 // 4, T % 4)
            if 8 <= T < 14:
                gather(T + 2)

        first = [x_tile(0, t) for t in range(4)]
        for t in range(4):
            gather(t)
            next(first[t])
        for t in range(4):
            next(first[t])
        for t in range(4):
            next(first[t])
            if t == 0:
                w_q(0, 0)
        for t in range(4):
            rope_tile(0, t)

        for n in range(FIRST, end):
            m = n - 5
            last = n > PAIRS + 1 and n in ffn_slots
            if last:
                tile = ffn_tile(ffn_slots[n])
                next(tile)
                next(tile)
            if 0 <= n - 9 < PAIRS:
                accumulate(n - 9)
            staged = []
            if n in ffn_slots and not last:
                staged.append(ffn_tile(ffn_slots[n]))
            if n in x_slots:
                T = x_slots[n]
                staged.append(x_tile(16 * (T // 8) + T % 8 // 4, T % 4))
            assert len(staged) < 2
            if staged:
                next(staged[0])
            early = jobs.get(n, [])
            for job in [q for q in early if q[0] is w_o and q[2] >= 2]:
                job[0](*job[1:])
            if 0 <= n < PAIRS:
                project_q(n)
            if 0 <= m < PAIRS:
                scores(m)
                soft_max(m)
            for part in staged:
                next(part)
            if 0 <= m - 1 < PAIRS:
                turn_p(m - 1)
                turned_p(m - 1)
                turned_pl(m - 1)
                turned_px(m - 1)
            if 0 <= m - 2 < PAIRS:
                values(m - 2)
                attended(m - 2)
                attended_l(m - 2)
            if 0 <= m < PAIRS:
                exponent(m)
                divide(m)
            if n - 1 > PAIRS and n - 1 in ffn_slots:
                ffn(ffn_slots[n - 1])
            if last:
                next(tile)
            for job in [q for q in early if not (q[0] is w_o and q[2] >= 2)]:
                job[0](*job[1:])
            if n < 0:
                gather(n + 8)
            if n == HALF - 5:
                gather(8)
                gather(9)
            if n in rope_slots:
                turn_rope(rope_slots[n])
            if 0 <= n < PAIRS and n % 4 == 1:
                project_k(n // 4)
            s, t = (n - 3) // 4, (n - 3) % 4
            if 0 <= s < STEPS and group_of(s) % 2 == 0:
                project_v(s, t)
            if n >= 10:
                for _ in range(3):
                    next(weights, None)
            if n - 1 in ffn_slots and n - 1 < PAIRS:
                ffn(ffn_slots[n - 1])
            if n in x_slots and x_slots[n] % 4 == 3 and len(staged) == 1:
                next(staged.pop())
            if 0 <= n - 8 < PAIRS:
                project_o(n - 8)
            for part in staged:
                next(part)
            if n == FIRST:
                for j in range(4, 8):
                    load_x(0, j)
            if HALF + 7 <= n < HALF + 15:
                load_x(1, n - HALF - 7)

        for T in (8 * (HALVES - 1) + j for j in range(8)):
            sp.add(None, lambda e: None, f"OUT{T}")

        block = ctx.enter_context(nc.Block())

        @block.sync
        def _(eng):
            P.issue(sp, eng)

        @block.tensor
        def _(eng):
            P.issue(pe, eng)

        @block.scalar
        def _(eng):
            P.issue(act, eng)

        @block.vector
        def _(eng):
            P.issue(dve, eng)

        @block.gpsimd
        def _(eng):
            P.issue(pool, eng)


def rope_table():
    inv = (np.float32(1.0) / np.float32(10000.0) ** (np.arange(0, 128, 2, dtype=np.float32) / np.float32(128)))
    f = np.arange(512, dtype=np.float32)[:, None] * inv.astype(np.float32)[None, :]
    c, s = np.cos(f), np.sin(f)
    return np.ascontiguousarray(np.concatenate([c, c, s, -s], axis=1).astype(np.float32))


def kernel(x, ctx_4096, pos_BxS2, mask_BxSxS2_ik0, L0_xattn_Wq, L0_xattn_Wk, L0_xattn_Wv, L0_xattn_Wo,
           L0_ffn_kernel, L0_ffn_bias):
    import concourse.bacc as _bacc
    from concourse.bass_utils import run_bass_kernel_spmd as _run

    nc = _bacc.Bacc("TRN2", target_bir_lowering=False, num_devices=1)
    c = np.ascontiguousarray
    wide = lambda w: c(np.asarray(w).reshape(4, 128, -1, 128).transpose(2, 1, 0, 3))
    arrays = {
        "x": c(np.asarray(x).reshape(16, 128, 512)),
        "ctxT": c(np.asarray(ctx_4096).reshape(16, 128, 4, 128).transpose(0, 3, 2, 1)),
        "pos": c(np.asarray(pos_BxS2).reshape(16, 128).T),
        "mask": c(np.asarray(mask_BxSxS2_ik0)),
        "wq": wide(L0_xattn_Wq),
        "wk": wide(L0_xattn_Wk),
        "wv": wide(L0_xattn_Wv),
        "wo": c(np.asarray(L0_xattn_Wo).reshape(32, 128, 512)),
        "fkT": c(np.asarray(L0_ffn_kernel).T.reshape(4, 128, 512)),
        "fbias": c(np.broadcast_to(np.asarray(L0_ffn_bias)[None, :], (128, 512))),
        "table": rope_table(),
        "eye": np.eye(128, dtype=np.float32),
    }
    aps = [nc.dram_tensor(n, a.shape, mybir.dt.from_np(a.dtype), kind="ExternalInput").ap() for n, a in arrays.items()]
    out = nc.dram_tensor("out", (16, 128, 512), F32, kind="ExternalOutput").ap()
    build(nc, *aps, out)
    r = _run(nc, [arrays], core_ids=[0])
    return np.asarray(r.results[0]["out"]).reshape(32, 64, 512)
```
